# Optimizing a Trainium2 kernel written in Bass

```python
import numpy as np
import jax
import jax.numpy as jnp

def _softmax(x, axis=-1):
    return jax.nn.softmax(x, axis=axis)

def _gelu(x):
    return jax.nn.gelu(x, approximate=True)

def _silu(x):
    return jax.nn.silu(x)

def _sigmoid(x):
    return jax.nn.sigmoid(x)

def _layernorm(x, axis=-1, eps=1e-05):
    m = jnp.mean(x, axis=axis, keepdims=True)
    v = jnp.var(x, axis=axis, keepdims=True)
    return (x - m) / jnp.sqrt(v + eps)

def _scatter_add(tgt, idx, src, axis=0):
    return tgt.at[idx].add(src)

def _segment_sum(src, seg, n):
    return jax.ops.segment_sum(src, seg, n)
kernel_name = 'mk_macaron_d1_jaxref_r8_72c62c'

def setup_inputs(seed: int=0):
    np.random.seed(seed)
    _w = jnp.asarray

    def _L0_attn_setup():
        import jax, jax.numpy as jnp
        import numpy as np
        BLOCK = 32
        NUM_HEADS = 16
        HEAD_DIM = 128
        FP4_GRID = jnp.array([0.0, 0.5, 1.0, 1.5, 2.0, 3.0, 4.0, 6.0], dtype=jnp.float32)

        def quantize_to_mxfp4(w, block_size=BLOCK):
            D, F = w.shape
            blocks = w.reshape(D // block_size, block_size, F)
            amax = jnp.max(jnp.abs(blocks), axis=1)
            e = jnp.floor(jnp.log2(jnp.maximum(amax, 1e-12) / 6.0))
            scale = jnp.exp2(e)
            v = blocks / scale[:, None, :]
            idx = jnp.argmin(jnp.abs(jnp.abs(v)[..., None] - FP4_GRID), axis=-1)
            codes = jnp.sign(v) * FP4_GRID[idx]
            return (codes.reshape(D, F).astype(jnp.float32), scale.astype(jnp.float32))

        def _mxfp4_matmul(x, codes, scales, block_size=BLOCK):
            w = codes * jnp.repeat(scales, block_size, axis=0)
            return x @ w
        key = jax.random.key(seed)
        ks = jax.random.split(key, 9)
        B, S, D = (2, 256, 256)
        feat = NUM_HEADS * HEAD_DIM
        x = jax.random.normal(ks[0], (B, S, D), dtype=jnp.float32)

        def make_w(k, din, dout):
            w = jax.random.normal(k, (din, dout), dtype=jnp.float32) * (1.0 / np.sqrt(din))
            return quantize_to_mxfp4(w, BLOCK)
        wq_codes, wq_scales = make_w(ks[1], D, feat)
        wk_codes, wk_scales = make_w(ks[2], D, feat)
        wv_codes, wv_scales = make_w(ks[3], D, feat)
        wo_codes, wo_scales = make_w(ks[4], feat, D)
        bq = jnp.zeros((feat,), jnp.float32)
        bk = jnp.zeros((feat,), jnp.float32)
        bv = jnp.zeros((feat,), jnp.float32)
        bo = jnp.zeros((D,), jnp.float32)
        return {'x': x, 'wq_codes': wq_codes, 'wq_scales': wq_scales, 'bq': bq, 'wk_codes': wk_codes, 'wk_scales': wk_scales, 'bk': bk, 'wv_codes': wv_codes, 'wv_scales': wv_scales, 'bv': bv, 'wo_codes': wo_codes, 'wo_scales': wo_scales, 'bo': bo}
    _L0_attn_in = _L0_attn_setup()

    def _L0_ffn_setup():
        import jax, jax.numpy as jnp
        import numpy as np
        B, S, D = (2, 256, 256)
        E, TOP_K = (16, 2)
        F_EXP, F_SH = (128, 256)

        def _reference_tuple_inner(hidden_states, router_w, gate_w, up_w, down_w, shared_gate_w, shared_up_w, shared_down_w):
            b, s, d = hidden_states.shape
            flat = hidden_states.reshape(-1, d)
            T = flat.shape[0]
            router_logits = flat @ router_w.T
            probs = jax.nn.softmax(router_logits, axis=-1)
            topk_w, topk_idx = jax.lax.top_k(probs, TOP_K)
            topk_w = topk_w / jnp.sum(topk_w, axis=-1, keepdims=True)
            shared = jax.nn.silu(flat @ shared_gate_w) * (flat @ shared_up_w) @ shared_down_w
            flat_idx = topk_idx.reshape(-1)
            flat_w = topk_w.reshape(-1)
            token_ids = jnp.repeat(jnp.arange(T), TOP_K)
            order = jnp.argsort(flat_idx)
            sorted_tok = token_ids[order]
            sorted_w = flat_w[order]
            group_sizes = jnp.bincount(flat_idx, length=E).astype(jnp.int32)
            xs = flat[sorted_tok]
            g = jax.lax.ragged_dot(xs, gate_w, group_sizes)
            u = jax.lax.ragged_dot(xs, up_w, group_sizes)
            h = jax.nn.silu(g) * u
            dn = jax.lax.ragged_dot(h, down_w, group_sizes)
            routed = jnp.zeros_like(flat).at[sorted_tok].add(sorted_w[:, None] * dn)
            output = (shared + routed).reshape(b, s, d)
            return (output, router_logits)
        key = jax.random.key(seed)
        ks = jax.random.split(key, 8)
        scale = 0.02
        return {'hidden_states': jax.random.normal(ks[0], (B, S, D), jnp.float32), 'router_w': jax.random.normal(ks[1], (E, D), jnp.float32) * scale, 'gate_w': jax.random.normal(ks[2], (E, D, F_EXP), jnp.float32) * scale, 'up_w': jax.random.normal(ks[3], (E, D, F_EXP), jnp.float32) * scale, 'down_w': jax.random.normal(ks[4], (E, F_EXP, D), jnp.float32) * scale, 'shared_gate_w': jax.random.normal(ks[5], (D, F_SH), jnp.float32) * scale, 'shared_up_w': jax.random.normal(ks[6], (D, F_SH), jnp.float32) * scale, 'shared_down_w': jax.random.normal(ks[7], (F_SH, D), jnp.float32) * scale}
    _L0_ffn_in = _L0_ffn_setup()
    _d = {'L0_attn_x': _L0_attn_in['x'], 'L0_attn_wq_codes': _L0_attn_in['wq_codes'], 'L0_attn_wq_scales': _L0_attn_in['wq_scales'], 'L0_attn_bq': _L0_attn_in['bq'], 'L0_attn_wk_codes': _L0_attn_in['wk_codes'], 'L0_attn_wk_scales': _L0_attn_in['wk_scales'], 'L0_attn_bk': _L0_attn_in['bk'], 'L0_attn_wv_codes': _L0_attn_in['wv_codes'], 'L0_attn_wv_scales': _L0_attn_in['wv_scales'], 'L0_attn_bv': _L0_attn_in['bv'], 'L0_attn_wo_codes': _L0_attn_in['wo_codes'], 'L0_attn_wo_scales': _L0_attn_in['wo_scales'], 'L0_attn_bo': _L0_attn_in['bo'], 'L0_ffn_router_w': _L0_ffn_in['router_w'], 'L0_ffn_gate_w': _L0_ffn_in['gate_w'], 'L0_ffn_up_w': _L0_ffn_in['up_w'], 'L0_ffn_down_w': _L0_ffn_in['down_w'], 'L0_ffn_shared_gate_w': _L0_ffn_in['shared_gate_w'], 'L0_ffn_shared_up_w': _L0_ffn_in['shared_up_w'], 'L0_ffn_shared_down_w': _L0_ffn_in['shared_down_w']}
    _x0 = _d['L0_attn_x']
    _d['L0_attn_x'] = jax.random.normal(jax.random.fold_in(jax.random.key(seed), 1), (4, 512, 256), dtype=_x0.dtype)
    del _x0
    return _d

def reference(L0_attn_x, L0_attn_wq_codes, L0_attn_wq_scales, L0_attn_bq, L0_attn_wk_codes, L0_attn_wk_scales, L0_attn_bk, L0_attn_wv_codes, L0_attn_wv_scales, L0_attn_bv, L0_attn_wo_codes, L0_attn_wo_scales, L0_attn_bo, L0_ffn_router_w, L0_ffn_gate_w, L0_ffn_up_w, L0_ffn_down_w, L0_ffn_shared_gate_w, L0_ffn_shared_up_w, L0_ffn_shared_down_w):

    def _L0_attn_ref(x, wq_codes, wq_scales, bq, wk_codes, wk_scales, bk, wv_codes, wv_scales, bv, wo_codes, wo_scales, bo):
        import jax, jax.numpy as jnp
        import numpy as np
        BLOCK = 32
        NUM_HEADS = 16
        HEAD_DIM = 128
        FP4_GRID = jnp.array([0.0, 0.5, 1.0, 1.5, 2.0, 3.0, 4.0, 6.0], dtype=jnp.float32)

        def quantize_to_mxfp4(w, block_size=BLOCK):
            D, F = w.shape
            blocks = w.reshape(D // block_size, block_size, F)
            amax = jnp.max(jnp.abs(blocks), axis=1)
            e = jnp.floor(jnp.log2(jnp.maximum(amax, 1e-12) / 6.0))
            scale = jnp.exp2(e)
            v = blocks / scale[:, None, :]
            idx = jnp.argmin(jnp.abs(jnp.abs(v)[..., None] - FP4_GRID), axis=-1)
            codes = jnp.sign(v) * FP4_GRID[idx]
            return (codes.reshape(D, F).astype(jnp.float32), scale.astype(jnp.float32))

        def _mxfp4_matmul(x, codes, scales, block_size=BLOCK):
            w = codes * jnp.repeat(scales, block_size, axis=0)
            return x @ w
        B, S, D = x.shape
        q = _mxfp4_matmul(x, wq_codes, wq_scales) + bq
        k = _mxfp4_matmul(x, wk_codes, wk_scales) + bk
        v = _mxfp4_matmul(x, wv_codes, wv_scales) + bv
        q = q.reshape(B, S, NUM_HEADS, HEAD_DIM)
        k = k.reshape(B, S, NUM_HEADS, HEAD_DIM)
        v = v.reshape(B, S, NUM_HEADS, HEAD_DIM)
        scores = jnp.einsum('bqhd,bkhd->bhqk', q, k) / jnp.sqrt(jnp.float32(HEAD_DIM))
        attn = jax.nn.softmax(scores, axis=-1)
        out = jnp.einsum('bhqk,bkhd->bqhd', attn, v).reshape(B, S, NUM_HEADS * HEAD_DIM)
        return _mxfp4_matmul(out, wo_codes, wo_scales) + bo

    def _L0_ffn_ref(hidden_states, router_w, gate_w, up_w, down_w, shared_gate_w, shared_up_w, shared_down_w):
        import jax, jax.numpy as jnp
        import numpy as np
        B, S, D = (2, 256, 256)
        E, TOP_K = (16, 2)
        F_EXP, F_SH = (128, 256)

        def _reference_tuple_inner(hidden_states, router_w, gate_w, up_w, down_w, shared_gate_w, shared_up_w, shared_down_w):
            b, s, d = hidden_states.shape
            flat = hidden_states.reshape(-1, d)
            T = flat.shape[0]
            router_logits = flat @ router_w.T
            probs = jax.nn.softmax(router_logits, axis=-1)
            topk_w, topk_idx = jax.lax.top_k(probs, TOP_K)
            topk_w = topk_w / jnp.sum(topk_w, axis=-1, keepdims=True)
            shared = jax.nn.silu(flat @ shared_gate_w) * (flat @ shared_up_w) @ shared_down_w
            flat_idx = topk_idx.reshape(-1)
            flat_w = topk_w.reshape(-1)
            token_ids = jnp.repeat(jnp.arange(T), TOP_K)
            order = jnp.argsort(flat_idx)
            sorted_tok = token_ids[order]
            sorted_w = flat_w[order]
            group_sizes = jnp.bincount(flat_idx, length=E).astype(jnp.int32)
            xs = flat[sorted_tok]
            g = jax.lax.ragged_dot(xs, gate_w, group_sizes)
            u = jax.lax.ragged_dot(xs, up_w, group_sizes)
            h = jax.nn.silu(g) * u
            dn = jax.lax.ragged_dot(h, down_w, group_sizes)
            routed = jnp.zeros_like(flat).at[sorted_tok].add(sorted_w[:, None] * dn)
            output = (shared + routed).reshape(b, s, d)
            return (output, router_logits)
        return _reference_tuple_inner(hidden_states, router_w, gate_w, up_w, down_w, shared_gate_w, shared_up_w, shared_down_w)[0]
    x = L0_attn_x
    x = x + 0.5 * _L0_ffn_ref(_layernorm(x, axis=-1), L0_ffn_router_w, L0_ffn_gate_w, L0_ffn_up_w, L0_ffn_down_w, L0_ffn_shared_gate_w, L0_ffn_shared_up_w, L0_ffn_shared_down_w)
    x = x + _L0_attn_ref(_layernorm(x, axis=-1), L0_attn_wq_codes, L0_attn_wq_scales, L0_attn_bq, L0_attn_wk_codes, L0_attn_wk_scales, L0_attn_bk, L0_attn_wv_codes, L0_attn_wv_scales, L0_attn_bv, L0_attn_wo_codes, L0_attn_wo_scales, L0_attn_bo)
    x = x + 0.5 * _L0_ffn_ref(_layernorm(x, axis=-1), L0_ffn_router_w, L0_ffn_gate_w, L0_ffn_up_w, L0_ffn_down_w, L0_ffn_shared_gate_w, L0_ffn_shared_up_w, L0_ffn_shared_down_w)
    return x

_drawn_inputs = setup_inputs


def setup_inputs(seed=0):
    import zlib

    import numpy as np

    out = dict(_drawn_inputs(seed))
    spreads = {'L0_attn_bq': (0.0, 0.8),
     'L0_attn_bk': (0.0, 0.8),
     'L0_attn_bv': (0.0, 0.1),
     'L0_attn_bo': (0.0, 0.1)}
    factors = {'L0_attn_wq_scales': 4.059,
     'L0_attn_wk_scales': 4.066,
     'L0_attn_wv_scales': 3.757,
     'L0_ffn_router_w': 7.428,
     'L0_ffn_gate_w': 6.953,
     'L0_ffn_up_w': 6.878,
     'L0_ffn_down_w': 6.869,
     'L0_ffn_shared_gate_w': 3.429,
     'L0_ffn_shared_up_w': 3.391,
     'L0_ffn_shared_down_w': 3.392}
    for name, (base, spread) in spreads.items():
        noise = np.random.default_rng([zlib.crc32(name.encode()), seed]).standard_normal(out[name].shape)
        drawn = base * np.exp(spread * noise) if base else spread * noise
        out[name] = jnp.asarray(drawn.astype(out[name].dtype))
    for name, factor in factors.items():
        out[name] = (out[name] * factor).astype(out[name].dtype)
    return out
```

```python
from contextlib import ExitStack

import concourse.bass as bass
from concourse import mybir

P = 128
F32 = mybir.dt.float32
F32R = mybir.dt.float32r
BF16 = mybir.dt.bfloat16
I32 = mybir.dt.int32
ALU = mybir.AluOpType
ACT = mybir.ActivationFunctionType
AX_X = mybir.AxisListType.X

B, S, D = 4, 512, 256
NTOK = B * S
NT = NTOK // P
KT = D // P
H, HD = 16, 128
QB = S // P
NE, TOPK, FE, FS = 16, 2, 128, 256
HG = 4
NG = H // HG
UNITS = B * H
LN_EPS = 1e-5
SM_SCALE = float(HD) ** -0.5

NSLOT_TILES = (NTOK * TOPK + NE * (P - 1)) // P
NR = -(-NSLOT_TILES // 4) * 4

CHUNK = 512
W_SH = KT * 2 * FS + (FS // P) * D
W_EX = KT * 2 * FE + D
W_ALL = W_SH + NE * W_EX
NCHUNK = W_ALL // CHUNK
SH_CHUNKS = W_SH // CHUNK
GR = 4
STEP_CHUNKS = (NCHUNK - SH_CHUNKS) // QB

PART = 2 * HD
PARTS_G = 4 * HG
NPARTS = NG * PARTS_G

C_ID, C_TRI, C_ONE, C_REV, C_J, C_LT, C_I = 0, 128, 256, 384, 400, 416, 672
C_N = C_I + NR

def wait(eng, sem, value):
    if isinstance(value, int) and value <= 0:
        return
    eng.wait_ge(sem, value)


class Carver:

    def __init__(self, tensor, start=0):
        self.t, self.at = tensor, start

    def cut(self, words):
        a = self.t[:, self.at:self.at + words]
        self.at += words
        return a


def build(nc, t):
    with ExitStack() as ctx:
        def sb(name, shape, dt=F32):
            return ctx.enter_context(nc.sbuf_tensor(name, shape, dt))

        m = {"ctx": ctx}
        m["X"] = sb("X", [P, NT, D])
        m["R"] = sb("R", [P, 37888], F32R)
        m["work"] = sb("work", [P, 8704])
        m["cst"] = sb("cst", [P, C_N])
        m["tri"] = sb("tri", [P, P], BF16)
        m["one"] = sb("one", [P, P], BF16)
        m["stats"] = sb("stats", [P, NT, 6])
        m["mv"] = sb("mv", [P, NT, 2])
        m["ln"] = sb("ln", [P, 5, NT])
        m["bank"] = [ctx.enter_context(nc.psum_tensor(f"bank{i}", [P, 512], F32)) for i in range(8)]
        m["xs_dram"] = nc.dram_tensor("xs_dram", (NR * P, D), F32, kind="Internal").ap()
        m["dn_dram"] = nc.dram_tensor("dn_dram", (NR * P, D), F32, kind="Internal").ap()
        ffn_phase(nc, t, m, 0)
        attention_phase(nc, t, m)
        ffn_phase(nc, t, m, 1)


def layernorm_dve(nc, dve, m, xn, s, x_ready):
    X, stats, mv, ln = m["X"], m["stats"], m["mv"], m["ln"]
    if x_ready is not None:
        dve.wait_ge(x_ready, 16)
    for i in range(NT):
        nc.vector.bn_stats(stats[:, i, :], X[:, i, :]).then_inc(s["ln"], 1)
    dve.wait_ge(s["ln"], NT)
    for i in range(NT):
        nc.vector.bn_aggr(mv[:, i, :], stats[:, i, :]).then_inc(s["ln"], 1)
    dve.wait_ge(s["ln"], 2 * NT)
    ve, sq, r, a, b = (ln[:, i, :] for i in range(5))
    nc.vector.tensor_scalar(ve, mv[:, :, 1], LN_EPS, None, ALU.add).then_inc(s["var"], 1)
    dve.wait_ge(s["sqrt"], 1)
    n = 2 * NT
    for op in (lambda: nc.vector.reciprocal(r, sq),
               lambda: nc.vector.tensor_tensor(a, ve, r, ALU.mult),
               lambda: nc.vector.tensor_tensor(b, a, r, ALU.mult),
               lambda: nc.vector.tensor_scalar(a, b, -0.5, 1.5, ALU.mult, ALU.add),
               lambda: nc.vector.tensor_tensor(b, r, a, ALU.mult)):
        op().then_inc(s["ln"], 1)
        n += 1
        dve.wait_ge(s["ln"], n)
    for i in range(NT):
        nc.vector.tensor_scalar(xn[:, i, :], X[:, i, :], mv[:, i, 0:1], b[:, i:i + 1],
                                ALU.subtract, ALU.mult).then_inc(s["xn"], 1)


def layernorm_act(nc, act, m, s):
    act.wait_ge(s["var"], 1)
    nc.scalar.activation(m["ln"][:, 1, :], m["ln"][:, 0, :], ACT.Sqrt).then_inc(s["sqrt"], 1)


def transpose_pe(nc, pe, m, xn, s):
    ident = m["cst"][:, C_ID:C_ID + P]
    for n in range(QB * KT):
        q, kt = divmod(n, KT)
        wait(pe, s["xn"], 4 * q + 4)
        wait(pe, s["xt_lo"], n - 1)
        for i in range(4):
            last = nc.tensor.transpose(m["bank"][n % 2][:, i * P:(i + 1) * P],
                                       xn[:, 4 * q + i, kt * P:(kt + 1) * P], ident)
        last.then_inc(s["xt"], 1)


def transpose_act(nc, act, m, xT, s):
    for n in range(QB * KT):
        q, kt = divmod(n, KT)
        act.wait_ge(s["xt"], n + 1)
        nc.scalar.activation(xT[:, 0, kt, q * S:(q + 1) * S], m["bank"][n % 2][:], ACT.Copy)\
            .then_inc(s["xt_hi"], 1)


def transpose_dve(nc, dve, m, xT, s):
    for n in range(QB * KT):
        q, kt = divmod(n, KT)
        dve.wait_ge(s["xt_hi"], n + 1)
        nc.vector.tensor_tensor(xT[:, 1, kt, q * S:(q + 1) * S], m["bank"][n % 2][:],
                                xT[:, 0, kt, q * S:(q + 1) * S].bitcast(F32), ALU.subtract)\
            .then_inc(s["xt_lo"], 1)


def product(nc, out, pairs):
    n = len(pairs)
    for i, (ah, al, bh, bl) in enumerate(pairs):
        nc.tensor.matmul(out, ah, bh, start=(i == 0), stop=False)
        nc.tensor.matmul(out, ah, bl, start=False, stop=False)
        last = nc.tensor.matmul(out, al, bh, start=False, stop=(i == n - 1))
    return last


def ffn_phase(nc, t, m, f):
    X, bank, cst = m["X"], m["bank"], m["cst"]
    xs_dram, dn_dram = m["xs_dram"], m["dn_dram"]
    r = Carver(m["R"])
    W = [r.cut(W_ALL), r.cut(W_ALL)]
    xT = r.cut(2 * KT * NTOK).rearrange("p (l k n) -> p l k n", l=2, k=KT)
    small = r.at
    hT = r.cut(2 * 2 * S).rearrange("p (j l n) -> p j l n", j=2, l=2)
    r = Carver(m["R"], small)
    xsT = r.cut(2 * 2 * KT * P).rearrange("p (b l k n) -> p b l k n", b=2, l=2, k=KT)
    hrT = r.cut(2 * 2 * P).rearrange("p (b l n) -> p b l n", b=2, l=2)
    w = Carver(m["work"])
    xn = w.cut(NT * D).rearrange("p (t d) -> p t d", t=NT)
    stg = w.cut(2 * CHUNK).rearrange("p (b n) -> p b n", b=2)
    small = w.at
    sg = w.cut(2 * S).rearrange("p (j n) -> p j n", j=2)
    hf = w.cut(S)
    w = Carver(m["work"], small)
    xs = w.cut(4 * D).rearrange("p (b d) -> p b d", b=4)
    dnb = w.cut(4 * D).rearrange("p (b d) -> p b d", b=4)
    sgr = w.cut(2 * P).rearrange("p (b n) -> p b n", b=2)
    hr = w.cut(2 * P).rearrange("p (b n) -> p b n", b=2)
    G = m["work"][:, small:small + GR * D].rearrange("p (b d) -> p b d", b=GR)
    te3 = lambda a: a.rearrange("p (t e) -> p t e", t=NT)
    L, oh1, oh2, tmp = te3(w.cut(256)), te3(w.cut(256)), te3(w.cut(256)), te3(w.cut(256))
    zero = dnb[:, 3, :]

    with ExitStack() as ctx:
        sems = {}

        def sem(name):
            sems[name] = m["ctx"].enter_context(nc.semaphore(f"f{f}_{name}"))
            return sems[name]

        def sb(name, shape, dt=F32):
            return ctx.enter_context(nc.sbuf_tensor(f"f{f}_{name}", shape, dt))

        A = sb("A", [P, NT + 1, NE], BF16)
        rt = sb("rt", [P, 8, NT])
        pos = [sb(f"pos{k}", [P, NT], I32) for k in range(TOPK)]
        wt = [sb(f"wt{k}", [P, NT]) for k in range(TOPK)]
        rwT = sb("rwT", [P, KT, NE])
        rw = sb("rw", [P, 2, KT, NE], F32R)
        ex = sb("ex", [P, 4, NE])
        te = sb("te", [1, NR], I32)
        tef = sb("tef", [1, NR])
        tec = sb("tec", [1, NR, NE])
        s = sems
        for name in ("x_in", "cst_in", "rw_in", "zeroed", "zfill", "tri", "ln", "var", "sqrt", "xn", "xt",
                     "xt_hi", "xt_lo", "rw", "logit", "route", "dlt", "e2", "hot", "rank", "pos",
                     "w_hi", "w_lo", "gu", "silu", "h", "h_hi", "h_lo", "dn", "x_add",
                     "scat", "r_xt", "r_xhi", "r_xlo", "r_gu", "r_silu", "r_h", "r_ht", "r_hhi", "r_hlo",
                     "r_dn", "r_ev0", "r_ev1", "comb"):
            if f == 0 or name not in ("x_in", "cst_in", "zeroed", "zfill", "tri"):
                sem(name)
        w_in = [sem(f"w_in{i}") for i in range(2)]
        xs_in = [sem(f"xs_in{i}") for i in range(4)]
        dn_out = [sem(f"dn_out{i}") for i in range(4)]
        g_in = [sem(f"g_in{i}") for i in range(GR)]
        if f == 1:
            sem("out")
        block = ctx.enter_context(nc.Block())

        ident = cst[:, C_ID:C_ID + P]

        def slots(eng, slot):
            for c in range(-1, 8):
                slot(0, c)
            with eng.Fori(2, NR // 4 - 1) as j:
                for c in range(4):
                    slot(j, c)
            for c in range(NR - 4, NR + 2):
                slot(0, c)

        def tiles(eng, do):
            for c in range(4):
                do(0, c)
            with eng.Fori(1, NR // 4) as j:
                for c in range(4):
                    do(j, c)

        def live(j, c):
            return not isinstance(j, int) or 0 <= 4 * j + c < NR

        def evac_dn(ns, eng, j, c):
            n = 4 * j + c
            eng.wait_ge(s["r_dn"], n + 1)
            wait(eng, dn_out[c % 4], 16 * (j + c // 4))
            if ns is nc.scalar:
                ins = nc.scalar.activation(dnb[:, c % 4, :], bank[6 + c % 2][:, 0:D], ACT.Copy)
            else:
                ins = nc.vector.tensor_copy(dnb[:, c % 4, :], bank[6 + c % 2][:, 0:D])
            ins.then_inc(s[f"r_ev{c % 2}"], 1)

        @block.sync
        def _(sp):
            if f == 0:
                sp.dma_start(X[:], t["x"].rearrange("(t p) d -> p t d", p=P)).then_inc(s["x_in"], 16)
                sp.dma_start(cst[:], t["consts"]).then_inc(s["cst_in"], 16)
            sp.dma_start(rwT[:], t["router"].rearrange("p (k e) -> p k e", k=KT)).then_inc(s["rw_in"], 16)

            def chunk(c, q, b):
                wait(sp, s["w_lo"], c - 1)
                sp.dma_start(stg[:, b, :], t["ffn_w"][:, bass.ds(c * CHUNK, CHUNK)]).then_inc(w_in[b], 16)

            chunk(0, 0, 0)
            chunk(1, 0, 1)
            if f == 0:
                sp.wait_ge(s["zeroed"], 1)
                sp.dma_start(xs_dram.rearrange("(p n) d -> p n d", p=P),
                             zero.unsqueeze(1).broadcast_to([P, NR, D])).then_inc(s["zfill"], 16)
            for c in range(2, 3):
                chunk(c, 0, c % 2)
            with sp.Fori(0, (NCHUNK - 3) // 2) as j:
                for b in range(2):
                    chunk(j * 2 + (3 + b), 0, (3 + b) % 2)

            sp.wait_ge(s["scat"], 16 * NT * TOPK)
            sp.wait_ge(s["x_add"], NT)

            def move(j, c):
                if live(j, c):
                    wait(sp, s["r_xt"], 4 * j + c - 3)
                    sp.dma_start(xs[:, c % 4, :], xs_dram[bass.ds((4 * j + c) * P, P), :])\
                        .then_inc(xs_in[c % 4], 16)
                if live(j, c - 4):
                    n = 4 * j + (c - 4)
                    wait(sp, s[f"r_ev{c % 2}"], 2 * j + (c - 4) // 2 + 1)
                    sp.dma_start(dn_dram[bass.ds(n * P, P), :], dnb[:, c % 4, :]).then_inc(dn_out[c % 4], 16)

            for c in range(4):
                move(0, c)
            with sp.Fori(1, NR // 4) as j:
                for c in range(4):
                    move(j, c)
            for c in range(NR, NR + 4):
                move(0, c)
            if f == 1:
                out_v = t["out"].rearrange("(t p) d -> p t d", p=P)
                for q in range(QB):
                    sp.wait_ge(s["comb"], TOPK * 4 * (q + 1))
                    sp.dma_start(out_v[:, 4 * q:4 * q + 4, :], X[:, 4 * q:4 * q + 4, :]).then_inc(s["out"], 16)
                sp.wait_ge(s["out"], 16 * QB)

        @block.gpsimd
        def _(pool):
            if f == 0:
                nc.gpsimd.memset(zero, 0.0).then_inc(s["zeroed"], 1)
                pool.wait_ge(s["zfill"], 16)
            for i in range(NT):
                for k in range(TOPK):
                    if i == 0:
                        pool.wait_ge(s["pos"], k + 1)
                    if i == 0 and k == 0:
                        pool.wait_ge(s["xn"], NT)
                    nc.gpsimd.indirect_dma_start(
                        out=xs_dram, out_offset=bass.IndirectOffsetOnAxis(ap=pos[k][:, i:i + 1], axis=0),
                        in_=xn[:, i, :], in_offset=None).then_inc(s["scat"], 16)
            for i in range(4):
                pool.wait_ge(dn_out[i], 16 * (NR // 4))
            pool.wait_ge(s["r_ev0"], NR // 2)
            pool.wait_ge(s["r_ev1"], NR // 2)
            for n in range(NT * TOPK):
                i, k = divmod(n, TOPK)
                wait(pool, s["comb"], n - GR + 1)
                nc.gpsimd.indirect_dma_start(
                    out=G[:, n % GR, :], out_offset=None, in_=dn_dram,
                    in_offset=bass.IndirectOffsetOnAxis(ap=pos[k][:, i:i + 1], axis=0)).then_inc(g_in[n % GR], 16)

        @block.scalar
        def _(act):
            layernorm_act(nc, act, m, s)
            act.wait_ge(s["rw_in"], 16)
            nc.scalar.activation(rw[:, 0], rwT[:], ACT.Copy).then_inc(s["rw"], 1)
            transpose_act(nc, act, m, xT, s)

            def split_hi(c, q, b):
                act.wait_ge(w_in[b], (q + 1) * 16)
                nc.scalar.activation(W[0][:, bass.ds(c * CHUNK, CHUNK)], stg[:, b, :], ACT.Copy)\
                    .then_inc(s["w_hi"], 1)

            for c in range(SH_CHUNKS):
                split_hi(c, c // 2, c % 2)
            act.wait_ge(s["dlt"], 1)
            nc.scalar.activation(rt[:, 5, :], rt[:, 4, :], ACT.Exp).then_inc(s["e2"], 1)

            def shared(step):
                for j in range(2):
                    k = step * 2 + j
                    act.wait_ge(s["gu"], k + 1)
                    wait(act, s["h"], k - 1)
                    nc.scalar.activation(sg[:, j, :], bank[j][:], ACT.Silu).then_inc(s["silu"], 1)
                    act.wait_ge(s["h"], k + 1)
                    wait(act, s["dn"], step * 4)
                    nc.scalar.activation(hT[:, j, 0, :], hf, ACT.Copy).then_inc(s["h_hi"], 1)
                for c in range(STEP_CHUNKS):
                    n = SH_CHUNKS + c
                    split_hi(step * STEP_CHUNKS + n, step * (STEP_CHUNKS // 2) + n // 2, n % 2)

            shared(0)
            with act.Fori(1, QB) as step:
                shared(step)
            act.wait_ge(s["x_add"], NT)

            def slot(j, c):
                i = 4 * j + c
                if live(j, c + 1):
                    act.wait_ge(s["r_xt"], i + 2)
                    wait(act, s["r_gu"], i)
                    nc.scalar.activation(xsT[:, (c + 1) % 2, 0].rearrange("p k n -> p (k n)"),
                                         bank[(c + 1) % 2][:, 0:D], ACT.Copy).then_inc(s["r_xhi"], 1)
                if live(j, c):
                    act.wait_ge(s["r_gu"], i + 1)
                    wait(act, s["r_h"], i - 1)
                    nc.scalar.activation(sgr[:, c % 2, :], bank[2 + c % 2][:, 0:FE], ACT.Silu)\
                        .then_inc(s["r_silu"], 1)
                if live(j, c - 1):
                    act.wait_ge(s["r_ht"], i)
                    wait(act, s["r_dn"], i - 2)
                    nc.scalar.activation(hrT[:, (c - 1) % 2, 0, :], bank[4 + (c - 1) % 2][:, 0:P], ACT.Copy)\
                        .then_inc(s["r_hhi"], 1)
                if live(j, c - 2) and c % 2 == 0:
                    evac_dn(nc.scalar, act, j, c - 2)

            slots(act, slot)

        @block.vector
        def _(dve):
            if f == 0:
                dve.wait_ge(s["cst_in"], 16)
                nc.vector.tensor_copy(m["tri"][:], cst[:, C_TRI:C_TRI + P])
                nc.vector.tensor_copy(m["one"][:], cst[:, C_ONE:C_ONE + P]).then_inc(s["tri"], 1)
            layernorm_dve(nc, dve, m, xn, s, s["x_in"] if f == 0 else None)
            dve.wait_ge(s["rw"], 1)
            nc.vector.tensor_tensor(rw[:, 1], rwT[:], rw[:, 0].bitcast(F32), ALU.subtract).then_inc(s["rw"], 1)
            transpose_dve(nc, dve, m, xT, s)

            def split_lo(c, b):
                dve.wait_ge(s["w_hi"], c + 1)
                nc.vector.tensor_tensor(W[1][:, bass.ds(c * CHUNK, CHUNK)], stg[:, b, :],
                                        W[0][:, bass.ds(c * CHUNK, CHUNK)].bitcast(F32), ALU.subtract)\
                    .then_inc(s["w_lo"], 1)

            for c in range(SH_CHUNKS):
                split_lo(c, c % 2)

            n = [0]

            def link(ins):
                ins.then_inc(s["route"], 1)
                n[0] += 1
                dve.wait_ge(s["route"], n[0])

            rev = cst[:, C_REV:C_REV + NE].unsqueeze(1).broadcast_to([P, NT, NE])
            m1, r1, m2, r2, dl, e2, w1 = (rt[:, i, :] for i in range(7))
            wide = lambda a: a.unsqueeze(2).broadcast_to([P, NT, NE])
            nc.vector.memset(A[:, 0, :], 0.0)
            dve.wait_ge(s["logit"], 1)
            link(nc.vector.tensor_copy(L, te3(bank[2][:, 0:256])))
            link(nc.vector.reduce_max(m1, L, AX_X))
            link(nc.vector.tensor_tensor(tmp, L, wide(m1), ALU.is_equal))
            link(nc.vector.tensor_tensor(tmp, tmp, rev, ALU.mult))
            link(nc.vector.reduce_max(r1, tmp, AX_X))
            link(nc.vector.tensor_tensor(oh1, rev, wide(r1), ALU.is_equal))
            link(nc.vector.scalar_tensor_tensor(out=L, in0=oh1, scalar=-3.0e38, in1=L, op0=ALU.mult, op1=ALU.add))
            link(nc.vector.reduce_max(m2, L, AX_X))
            nc.vector.tensor_tensor(dl, m2, m1, ALU.subtract).then_inc(s["dlt"], 1)
            link(nc.vector.tensor_tensor(tmp, L, wide(m2), ALU.is_equal))
            link(nc.vector.tensor_tensor(tmp, tmp, rev, ALU.mult))
            link(nc.vector.reduce_max(r2, tmp, AX_X))
            link(nc.vector.tensor_tensor(oh2, rev, wide(r2), ALU.is_equal))
            nc.vector.tensor_tensor(A[:, 1:, :], oh1, oh2, ALU.add).then_inc(s["hot"], 1)
            dve.wait_ge(s["e2"], 1)
            link(nc.vector.tensor_scalar(w1, e2, 1.0, None, ALU.add))
            link(nc.vector.reciprocal(r1, w1))
            link(nc.vector.tensor_scalar(wt[0][:], r1, 0.5, None, ALU.mult))
            link(nc.vector.tensor_tensor(wt[1][:], wt[0][:], e2, ALU.mult))
            dve.wait_ge(s["rank"], 1)
            cnt = ex[:, 0, :]
            link(nc.vector.tensor_copy(cnt, bank[3][:, 256:256 + NE]))
            jj = cst[:, C_J:C_J + NE].unsqueeze(1).broadcast_to([P, NE, NE])
            lt = cst[:, C_LT:C_LT + NE * NE].rearrange("p (a b) -> p a b", a=NE)
            link(nc.vector.tensor_tensor(tmp, cnt.unsqueeze(2).broadcast_to([P, NE, NE]), jj, ALU.is_gt))
            link(nc.vector.reduce_sum(ex[:, 1, :], tmp, AX_X))
            link(nc.vector.tensor_tensor(tmp, ex[:, 1, :].unsqueeze(1).broadcast_to([P, NE, NE]), lt, ALU.mult))
            link(nc.vector.reduce_sum(ex[:, 2, :], tmp, AX_X))
            link(nc.vector.tensor_scalar(ex[:, 3, :], ex[:, 2, :], float(P), None, ALU.mult))
            link(nc.vector.tensor_tensor(tmp, te3(bank[3][:, 0:256]),
                                         ex[:, 3, :].unsqueeze(1).broadcast_to([P, NT, NE]), ALU.add))
            for k, oh in enumerate((oh1, oh2)):
                link(nc.vector.tensor_tensor(oh, oh, tmp, ALU.mult))
                link(nc.vector.reduce_sum(rt[:, k, :], oh, AX_X))
                nc.vector.tensor_copy(pos[k][:], rt[:, k, :]).then_inc(s["pos"], 1)
            link(nc.vector.tensor_tensor(ex[:, 0, :], ex[:, 1, :], ex[:, 2, :], ALU.add))
            link(nc.vector.tensor_tensor(tec[:], ex[0:1, 0, :].unsqueeze(1).broadcast_to([1, NR, NE]),
                                         cst[0:1, C_I:C_I + NR].unsqueeze(2).broadcast_to([1, NR, NE]), ALU.is_le))
            link(nc.vector.reduce_sum(tef[:], tec[:], AX_X))
            nc.vector.tensor_scalar(te[:], tef[:], float(NE - 1), None, ALU.min).then_inc(s["pos"], 1)

            def shared(step):
                for j in range(2):
                    k = step * 2 + j
                    dve.wait_ge(s["silu"], k + 1)
                    wait(dve, s["h_lo"], k)
                    nc.vector.tensor_tensor(hf, bank[4 + j][:], sg[:, j, :], ALU.mult).then_inc(s["h"], 1)
                    dve.wait_ge(s["h_hi"], k + 1)
                    nc.vector.tensor_tensor(hT[:, j, 1, :], hf, hT[:, j, 0, :].bitcast(F32), ALU.subtract)\
                        .then_inc(s["h_lo"], 1)
                for q in range(QB):
                    dve.wait_ge(s["dn"], step * 4 + (q + 1))
                    xi = X[:, bass.ds(step * 4 + q, 1), :].rearrange("p a d -> p (a d)")
                    nc.vector.scalar_tensor_tensor(out=xi, in0=bank[6 + q % 2][:, 0:D], scalar=0.5, in1=xi,
                                                   op0=ALU.mult, op1=ALU.add).then_inc(s["x_add"], 1)
                for c in range(STEP_CHUNKS):
                    split_lo(step * STEP_CHUNKS + (SH_CHUNKS + c), (SH_CHUNKS + c) % 2)

            shared(0)
            with dve.Fori(1, QB) as step:
                shared(step)

            def slot(j, c):
                i = 4 * j + c
                if live(j, c + 1):
                    dve.wait_ge(s["r_xhi"], i + 2)
                    nc.vector.tensor_tensor(xsT[:, (c + 1) % 2, 1].rearrange("p k n -> p (k n)"),
                                            bank[(c + 1) % 2][:, 0:D],
                                            xsT[:, (c + 1) % 2, 0].rearrange("p k n -> p (k n)").bitcast(F32),
                                            ALU.subtract).then_inc(s["r_xlo"], 1)
                if live(j, c):
                    dve.wait_ge(s["r_silu"], i + 1)
                    wait(dve, s["r_ht"], i - 1)
                    nc.vector.tensor_tensor(hr[:, c % 2, :], bank[2 + c % 2][:, FE:2 * FE], sgr[:, c % 2, :],
                                            ALU.mult).then_inc(s["r_h"], 1)
                if live(j, c - 1):
                    dve.wait_ge(s["r_hhi"], i)
                    nc.vector.tensor_tensor(hrT[:, (c - 1) % 2, 1, :], bank[4 + (c - 1) % 2][:, 0:P],
                                            hrT[:, (c - 1) % 2, 0, :].bitcast(F32), ALU.subtract)\
                        .then_inc(s["r_hlo"], 1)
                if live(j, c - 2) and c % 2 == 1:
                    evac_dn(nc.vector, dve, j, c - 2)

            slots(dve, slot)
            for k in range(NT * TOPK):
                i, kk = divmod(k, TOPK)
                dve.wait_ge(g_in[k % GR], 16 * (k // GR + 1))
                wait(dve, s["comb"], k)
                nc.vector.scalar_tensor_tensor(out=X[:, i, :], in0=G[:, k % GR, :], scalar=wt[kk][:, i:i + 1],
                                               in1=X[:, i, :], op0=ALU.mult, op1=ALU.add).then_inc(s["comb"], 1)

        @block.tensor
        def _(pe):
            if f == 0:
                pe.wait_ge(s["cst_in"], 16)
            transpose_pe(nc, pe, m, xn, s)
            pe.wait_ge(s["xt_lo"], QB * KT)
            pe.wait_ge(s["rw"], 2)
            for i in range(NT):
                last = product(nc, bank[2][:, i * NE:(i + 1) * NE],
                               [(xT[:, 0, kt, i * P:(i + 1) * P], xT[:, 1, kt, i * P:(i + 1) * P],
                                 rw[:, 0, kt, :], rw[:, 1, kt, :]) for kt in range(KT)])
            last.then_inc(s["logit"], 1)

            wv = [w_[:, 0:W_SH - 2 * D].rearrange("p (k g n) -> p k g n", k=KT, g=2) for w_ in W]
            wd = [w_[:, W_SH - 2 * D:W_SH].rearrange("p (j n) -> p j n", j=2) for w_ in W]

            def gate_up(step, j):
                k = step * 2 + j
                wait(pe, s["h"], k - 1)
                for g, out in ((0, bank[j]), (1, bank[4 + j])):
                    last = product(nc, out[:], [(wv[0][:, kt, g, j * P:(j + 1) * P], wv[1][:, kt, g, j * P:(j + 1) * P],
                                                 xT[:, 0, kt, bass.ds(step * S, S)],
                                                 xT[:, 1, kt, bass.ds(step * S, S)]) for kt in range(KT)])
                last.then_inc(s["gu"], 1)

            def down(step):
                pe.wait_ge(s["h_lo"], step * 2 + 2)
                for q in range(QB):
                    wait(pe, s["x_add"], step * 4 + (q - 1))
                    product(nc, bank[6 + q % 2][:, 0:D],
                            [(hT[:, j, 0, q * P:(q + 1) * P], hT[:, j, 1, q * P:(q + 1) * P],
                              wd[0][:, j, :], wd[1][:, j, :]) for j in range(2)]).then_inc(s["dn"], 1)

            pe.wait_ge(s["w_lo"], SH_CHUNKS)
            gate_up(0, 0)
            gate_up(0, 1)
            if f == 0:
                pe.wait_ge(s["tri"], 1)
            pe.wait_ge(s["hot"], 1)
            flatA = A[:].rearrange("p t e -> p (t e)")
            nc.tensor.matmul(bank[3][:, 0:256], m["tri"][:], flatA[:, NE:], start=True, stop=False)
            for back in range(NT - 1, 1, -1):
                nc.tensor.matmul(bank[3][:, back * NE:256], m["one"][:], flatA[:, NE:NE + 256 - back * NE],
                                 start=False, stop=False)
            nc.tensor.matmul(bank[3][:, 0:256], m["one"][:], flatA[:, 0:256], start=False, stop=True)
            for i in range(NT):
                last = nc.tensor.matmul(bank[3][:, 256:256 + NE], m["one"][:], A[:, i + 1, :],
                                        start=(i == 0), stop=(i == NT - 1))
            last.then_inc(s["rank"], 1)
            gate_up(1, 0)
            down(0)
            with pe.Fori(1, QB - 1) as step:
                gate_up(step, 1)
                gate_up(step + 1, 0)
                down(step)
            gate_up(QB - 1, 1)
            down(QB - 1)

            pe.wait_ge(s["w_lo"], NCHUNK)
            pe.wait_ge(s["pos"], 3)
            we = [w_[:, W_SH:W_ALL].rearrange("p (e n) -> p e n", e=NE) for w_ in W]

            def slot(j, c):
                i = 4 * j + c
                if live(j, c + 1):
                    b = (c + 1) % 2
                    pe.wait_ge(xs_in[(c + 1) % 4], 16 * (j + (c + 1) // 4 + 1))
                    wait(pe, s["r_xlo"], i)
                    for kt in range(KT):
                        last = nc.tensor.transpose(bank[b][:, kt * P:(kt + 1) * P],
                                                   xs[:, (c + 1) % 4, kt * P:(kt + 1) * P], ident)
                    last.then_inc(s["r_xt"], 1)
                if live(j, c):
                    b = c % 2
                    e = pe.value_load(te[0:1, bass.ds(i, 1)], min_val=0, max_val=NE - 1)
                    pe.wait_ge(s["r_xlo"], i + 1)
                    wait(pe, s["r_h"], i - 1)
                    gu = [[w_[:, bass.ds(e, 1), kt * 2 * FE:(kt + 1) * 2 * FE].rearrange("p a n -> p (a n)")
                           for w_ in we] for kt in range(KT)]
                    product(nc, bank[2 + b][:, 0:2 * FE],
                            [(xsT[:, b, 0, kt, :], xsT[:, b, 1, kt, :], gu[kt][0], gu[kt][1])
                             for kt in range(KT)]).then_inc(s["r_gu"], 1)
                if live(j, c - 1):
                    b = (c - 1) % 2
                    pe.wait_ge(s["r_h"], i)
                    wait(pe, s["r_hlo"], i - 2)
                    nc.tensor.transpose(bank[4 + b][:, 0:P], hr[:, b, :], ident).then_inc(s["r_ht"], 1)
                if live(j, c - 2):
                    b = c % 2
                    e = pe.value_load(te[0:1, bass.ds(i - 2, 1)], min_val=0, max_val=NE - 1)
                    pe.wait_ge(s["r_hlo"], i - 1)
                    wait(pe, s[f"r_ev{b}"], 2 * j + (c - 2) // 2)
                    d = [w_[:, bass.ds(e, 1), KT * 2 * FE:W_EX].rearrange("p a n -> p (a n)") for w_ in we]
                    product(nc, bank[6 + b][:, 0:D], [(hrT[:, b, 0, :], hrT[:, b, 1, :], d[0], d[1])])\
                        .then_inc(s["r_dn"], 1)

            slots(pe, slot)


def attention_phase(nc, t, m):
    X, bank, cst = m["X"], m["bank"], m["cst"]
    r = Carver(m["R"])
    xT = r.cut(2 * KT * NTOK).rearrange("p (l k n) -> p l k n", l=2, k=KT)
    vx = r.cut(4 * 2 * KT * P).rearrange("p (j l k n) -> p j l k n", j=4, l=2, k=KT)
    Wq, Wk, Wo = (r.cut(HG * 2 * PART).rearrange("p (h l n) -> p h l n", h=HG, l=2) for _ in range(3))
    Wv = r.cut(2 * 2 * KT * HG * HD).rearrange("p (g l k n) -> p g l k n", g=2, l=2, k=KT)
    V = r.cut(2 * 2 * QB * HG * HD).rearrange("p (i l b n) -> p i l b n", i=2, l=2, b=QB)
    qT = r.cut(2 * S).rearrange("p (l n) -> p l n", l=2)
    kT = r.cut(2 * S).rearrange("p (l n) -> p l n", l=2)
    PT = r.cut(2 * QB * S).rearrange("p (l b n) -> p l b n", l=2, b=QB)
    oT = r.cut(2 * S).rearrange("p (l n) -> p l n", l=2)
    assert r.at <= 37888
    w = Carver(m["work"])
    flat = w.cut(NT * D)
    xn = flat.rearrange("p (t d) -> p t d", t=NT)
    yT = flat.rearrange("p (o n) -> p o n", o=KT)
    Pm = w.cut(QB * S).rearrange("p (q n) -> p q n", q=QB)
    raw = w.cut(2 * 4 * PART).rearrange("p (c b n) -> p c b n", c=2, b=4)

    with ExitStack() as ctx:
        s = {}

        def sem(name):
            s[name] = m["ctx"].enter_context(nc.semaphore(f"a_{name}"))
            return s[name]

        def sb(name, shape, dt=F32):
            return ctx.enter_context(nc.sbuf_tensor(f"a_{name}", shape, dt))

        bias = sb("bias", [P, 3, H])
        bslot = sb("bslot", [P, HG, 3])
        bo = sb("bo", [P, KT])
        mx = sb("mx", [P, QB])
        sm = sb("sm", [P, QB])
        ri = sb("ri", [P, QB])
        for name in ("b_in", "ln", "var", "sqrt", "xn", "xt", "xt_hi", "xt_lo", "y0", "wstep", "wprep",
                     "q", "k", "v", "s", "t", "o", "y", "q_hi", "q_lo", "k_hi", "k_lo", "v_hi", "v_lo",
                     "max", "exp", "rsum", "norm", "t_hi", "t_lo", "o_hi", "o_lo", "y_add", "fin", "fin_add"):
            sem(name)
        raw_in = [sem(f"raw_in{i}") for i in range(4)]
        vx_in = [sem(f"vx_in{i}") for i in range(4)]
        block = ctx.enter_context(nc.Block())
        ident = cst[:, C_ID:C_ID + P]

        LOOP0, LOOP1 = 1, UNITS // 8 - 1

        def slots(eng, slot):
            for c in range(8 * LOOP0):
                slot(0, c)
            with eng.Fori(LOOP0, LOOP1) as j:
                for c in range(8):
                    slot(j, c)
            for c in range(8 * LOOP1, UNITS):
                slot(0, c)

        def it_of(j, c):
            return 2 * j + c // 4

        def batch_of(j, c):
            return it_of(j, c) % B

        def group_of(j, c):
            return it_of(j, c) // B

        def last(j, c):
            return isinstance(j, int) and 8 * j + c >= UNITS

        def load_vx(eng, n_it, jb, n):
            wait(eng, s["v"], n - 3)
            eng.dma_start(vx[:, jb].bitcast(F32).rearrange("p l k n -> p (l k) n"),
                          xT[:, :, :, bass.ds((n_it % B) * S + jb * P, P)].bitcast(F32)
                          .rearrange("p l k n -> p (l k) n")).then_inc(vx_in[jb], 16)

        @block.sync
        def _(sp):
            sp.dma_start(bias[:], t["attn_bias"].rearrange("p (a h) -> p a h", a=3)).then_inc(s["b_in"], 16)
            sp.dma_start(bo[:], t["bo"]).then_inc(s["b_in"], 16)

            def part(j, b):
                n = 4 * j + b
                wait(sp, s["wprep"], n - 3)
                sp.dma_start(raw[:, 0, b, :], t["codes"][bass.ds(n, 1), :, :].rearrange("a p n -> (a p) n"))\
                    .then_inc(raw_in[b], 16)
                for k in range(4):
                    sp.dma_start(raw[32 * k:32 * k + 32, 1, b, :],
                                 t["scales"][bass.ds(n, 1), k, :].broadcast_to([32, PART]))\
                        .then_inc(raw_in[b], 16)

            for b in range(4):
                part(0, b)
            with sp.Fori(1, NPARTS // 4) as j:
                for b in range(4):
                    part(j, b)

        @block.gpsimd
        def _(pool):
            pool.wait_ge(s["b_in"], 32)
            steps = [0]

            def link(ins):
                steps[0] += 1
                ins.then_inc(s["wstep"], 1)
                pool.wait_ge(s["wstep"], steps[0])

            link(nc.gpsimd.tensor_scalar(bias[:, 0, :], bias[:, 0, :], SM_SCALE, None, ALU.mult))
            n = 0
            for g in range(NG):
                for kind, hh in [("v", i) for i in range(HG)] + [(k, i) for i in range(HG) for k in "qko"]:
                    pool.wait_ge(raw_in[n % 4], 80 * (n // 4 + 1))
                    codes, scales = raw[:, 0, n % 4, :], raw[:, 1, n % 4, :]
                    if kind == "q":
                        link(nc.gpsimd.tensor_scalar(scales, scales, SM_SCALE, None, ALU.mult))
                    link(nc.gpsimd.tensor_tensor(codes, codes, scales, ALU.mult))
                    if kind == "v":
                        wait(pool, s["v"], 16 * g - 16)
                        hi, lo = (Wv[:, g % 2, l, :, hh * HD:(hh + 1) * HD] for l in range(2))
                        src = codes.rearrange("p (k n) -> p k n", k=KT)
                    else:
                        slot = {"q": Wq, "k": Wk, "o": Wo}[kind]
                        hi, lo = slot[:, hh, 0, :], slot[:, hh, 1, :]
                        src = codes
                        if kind in "qk":
                            wait(pool, s["k_lo"], 16 * g - 3 + hh)
                            if kind == "q" and g > 0:
                                pool.wait_ge(s["y"], 16 * g - 3 + hh)
                        else:
                            wait(pool, s["y"], 16 * g - 3 + hh)
                    if kind == "q":
                        link(nc.gpsimd.tensor_copy(bslot[:, hh, :], bias[:, :, 4 * g + hh]))
                    link(nc.gpsimd.tensor_copy(hi, src))
                    nc.gpsimd.tensor_tensor(lo, src, hi.bitcast(F32), ALU.subtract).then_inc(s["wprep"], 1)
                    n += 1

        @block.scalar
        def _(act):
            layernorm_act(nc, act, m, s)
            transpose_act(nc, act, m, xT, s)
            act.wait_ge(s["xt_lo"], QB * KT)
            for jb in range(4):
                load_vx(act, 0, jb, jb)

            def v_hi(n, jb, par, it):
                act.wait_ge(s["v"], n + 1)
                wait(act, s["o"], 4 * it - 4)
                nc.scalar.activation(V[:, par, 0, jb, :], bank[0][:], ACT.Copy).then_inc(s["v_hi"], 1)
                if not isinstance(n, int) or n + 4 < UNITS:
                    load_vx(act, it + 1, jb, n + 4)

            def qk_hi(bk, dst, pre, post, u1, hh, which):
                act.wait_ge(s[pre], u1)
                wait(act, s["s"], 4 * (u1 - 1))
                nc.scalar.activation(dst[:, 0, :], bank[bk][:], ACT.Identity, bias=bslot[:, hh, which:which + 1],
                                     scale=1.0).then_inc(s[post], 1)

            def exp_(u, qb):
                act.wait_ge(s["max"], 4 * u + (qb + 1))
                wait(act, s["t"], 4 * u)
                nc.scalar.activation(Pm[:, qb, :], bank[2 + qb % 2][:], ACT.Exp, bias=mx[:, qb:qb + 1], scale=1.0,
                                     accum_out=sm[:, qb:qb + 1]).then_inc(s["exp"], 1)

            def t_hi(u, kb):
                act.wait_ge(s["t"], 4 * u + (kb + 1))
                wait(act, s["o"], u)
                nc.scalar.activation(PT[:, 0, kb, :], bank[4 + kb % 2][:], ACT.Copy).then_inc(s["t_hi"], 1)

            for jb in range(4):
                v_hi(jb, jb, 0, 0)
            qk_hi(0, qT, "q", "q_hi", 1, 0, 0)
            qk_hi(1, kT, "k", "k_hi", 1, 0, 1)
            for qb in range(QB):
                exp_(0, qb)

            def slot(j, c):
                u = 8 * j + c
                more = not last(j, c + 1)
                if more:
                    qk_hi(0, qT, "q", "q_hi", u + 2, (c + 1) % 4, 0)
                t_hi(u, 0)
                if more:
                    qk_hi(1, kT, "k", "k_hi", u + 2, (c + 1) % 4, 1)
                t_hi(u, 1)
                if not last(j, c + 4):
                    v_hi(u + 4, c % 4, (c // 4 + 1) % 2, it_of(j, c + 4))
                t_hi(u, 2)
                t_hi(u, 3)
                if more:
                    for qb in range(QB):
                        exp_(u + 1, qb)
                act.wait_ge(s["o"], u + 1)
                wait(act, s["y"], u)
                nc.scalar.activation(oT[:, 0, :], bank[1][:], ACT.Identity, bias=bslot[:, c % 4, 2:3],
                                     scale=1.0).then_inc(s["o_hi"], 1)

            slots(act, slot)

        @block.vector
        def _(dve):
            layernorm_dve(nc, dve, m, xn, s, None)
            transpose_dve(nc, dve, m, xT, s)
            dve.wait_ge(s["b_in"], 32)
            nc.vector.memset(flat, 0.0).then_inc(s["y0"], 1)
            dve.wait_ge(s["y0"], 1)
            for o in range(KT):
                nc.vector.tensor_scalar(yT[:, o, :], yT[:, o, :], bo[:, o:o + 1], None, ALU.add).then_inc(s["y0"], 1)
            dve.wait_ge(s["y0"], 1 + KT)

            def v_lo(n, jb, par):
                dve.wait_ge(s["v_hi"], n + 1)
                nc.vector.tensor_tensor(V[:, par, 1, jb, :], bank[0][:], V[:, par, 0, jb, :].bitcast(F32),
                                        ALU.subtract).then_inc(s["v_lo"], 1)

            def bias_lo(bk, dst, pre, post, u1, hh, which):
                dve.wait_ge(s[pre], u1)
                nc.vector.scalar_tensor_tensor(out=dst[:, 1, :], in0=bank[bk][:], scalar=bslot[:, hh, which:which + 1],
                                               in1=dst[:, 0, :].bitcast(F32), op0=ALU.add, op1=ALU.subtract)\
                    .then_inc(s[post], 1)

            def max_(u, qb):
                dve.wait_ge(s["s"], 4 * u + (qb + 1))
                wait(dve, s["exp"], 4 * u + qb - 3)
                nc.vector.reduce_max(mx[:, qb:qb + 1], bank[2 + qb % 2][:], AX_X, negate=True)\
                    .then_inc(s["max"], 1)

            def norm(u, qb):
                dve.wait_ge(s["exp"], 4 * u + (qb + 1))
                nc.vector.reciprocal(ri[:, qb:qb + 1], sm[:, qb:qb + 1]).then_inc(s["rsum"], 1)
                dve.wait_ge(s["rsum"], 4 * u + (qb + 1))
                nc.vector.tensor_scalar(Pm[:, qb, :], Pm[:, qb, :], ri[:, qb:qb + 1], None, ALU.mult)\
                    .then_inc(s["norm"], 1)

            def t_lo(u, kb):
                dve.wait_ge(s["t_hi"], 4 * u + (kb + 1))
                nc.vector.tensor_tensor(PT[:, 1, kb, :], bank[4 + kb % 2][:], PT[:, 0, kb, :].bitcast(F32),
                                        ALU.subtract).then_inc(s["t_lo"], 1)

            def y_add(it, b):
                dve.wait_ge(s["y"], 4 * it + 4)
                wait(dve, s["y_add"], it)
                for o in range(KT):
                    yo = yT[:, o, bass.ds(b * S, S)]
                    ins = nc.vector.tensor_tensor(yo, bank[6 + o][:], yo, ALU.add)
                ins.then_inc(s["y_add"], 1)

            for jb in range(4):
                v_lo(jb, jb, 0)
            bias_lo(0, qT, "q_hi", "q_lo", 1, 0, 0)
            bias_lo(1, kT, "k_hi", "k_lo", 1, 0, 1)
            max_(0, 0)
            max_(0, 1)
            norm(0, 0)
            max_(0, 2)
            norm(0, 1)
            max_(0, 3)
            norm(0, 2)
            norm(0, 3)

            def slot(j, c):
                u = 8 * j + c
                more = not last(j, c + 1)
                if more:
                    bias_lo(0, qT, "q_hi", "q_lo", u + 2, (c + 1) % 4, 0)
                if c % 4 == 0 and not (isinstance(j, int) and u == 0):
                    y_add(it_of(j, c - 4), batch_of(j, c - 4 + 16) if not isinstance(j, int) else (u // 4 - 1) % B)
                t_lo(u, 0)
                if more:
                    bias_lo(1, kT, "k_hi", "k_lo", u + 2, (c + 1) % 4, 1)
                t_lo(u, 1)
                if not last(j, c + 4):
                    v_lo(u + 4, c % 4, (c // 4 + 1) % 2)
                t_lo(u, 2)
                if more:
                    max_(u + 1, 0)
                t_lo(u, 3)
                if more:
                    max_(u + 1, 1)
                    norm(u + 1, 0)
                    max_(u + 1, 2)
                    norm(u + 1, 1)
                    max_(u + 1, 3)
                    norm(u + 1, 2)
                    norm(u + 1, 3)
                bias_lo(1, oT, "o_hi", "o_lo", u + 1, c % 4, 2)

            slots(dve, slot)
            y_add(UNITS // 4 - 1, B - 1)
            for i in range(NT):
                dve.wait_ge(s["fin"], i + 1)
                nc.vector.tensor_tensor(X[:, i, :], bank[i % 2][:, 0:D], X[:, i, :], ALU.add)\
                    .then_inc(s["fin_add"], 1)

        @block.tensor
        def _(pe):
            transpose_pe(nc, pe, m, xn, s)
            pe.wait_ge(s["xt_lo"], QB * KT)

            def proj(Wx, bk, hh, tok, done):
                w_ = Wx[:, hh].rearrange("p l (k n) -> p l k n", k=KT)
                product(nc, bank[bk][:], [(w_[:, 0, kt, :], w_[:, 1, kt, :], xT[:, 0, kt, bass.ds(tok, S)],
                                           xT[:, 1, kt, bass.ds(tok, S)]) for kt in range(KT)]).then_inc(s[done], 1)

            def v_block(n, jb, it):
                wait(pe, s["wprep"], (it // B) * PARTS_G + HG)
                pe.wait_ge(vx_in[jb], 16 * it + 16)
                par = (it // B) % 2
                product(nc, bank[0][:], [(vx[:, jb, 0, kt, :], vx[:, jb, 1, kt, :],
                                          *(Wv[:, bass.ds(par, 1), l, kt, :].rearrange("p a n -> p (a n)")
                                            for l in range(2))) for kt in range(KT)]).then_inc(s["v"], 1)

            def scores(u, qb):
                wait(pe, s["exp"], 4 * u + qb - 1)
                q = slice(qb * P, (qb + 1) * P)
                product(nc, bank[2 + qb % 2][:], [(qT[:, 0, q], qT[:, 1, q], kT[:, 0, :], kT[:, 1, :])])\
                    .then_inc(s["s"], 1)

            def trans(u, kb):
                wait(pe, s["t_lo"], 4 * u + kb - 1)
                for qb in range(QB):
                    ins = nc.tensor.transpose(bank[4 + kb % 2][:, qb * P:(qb + 1) * P],
                                              Pm[:, qb, kb * P:(kb + 1) * P], ident)
                ins.then_inc(s["t"], 1)

            def pv(u, kb, c):
                pe.wait_ge(s["t_lo"], 4 * u + (kb + 1))
                hh, par = c % 4, (c // 4) % 2
                vh, vl = (V[:, par, l, kb, hh * HD:(hh + 1) * HD] for l in range(2))
                ph, pl = PT[:, 0, kb, :], PT[:, 1, kb, :]
                nc.tensor.matmul(bank[1][:], vh, ph, start=(kb == 0), stop=False)
                nc.tensor.matmul(bank[1][:], vh, pl, start=False, stop=False)
                ins = nc.tensor.matmul(bank[1][:], vl, ph, start=False, stop=(kb == QB - 1))
                if kb == QB - 1:
                    ins.then_inc(s["o"], 1)

            def out_proj(u, c):
                pe.wait_ge(s["o_lo"], u + 1)
                hh = c % 4
                if hh == 0:
                    wait(pe, s["y_add"], u // 4 if isinstance(u, int) else it_now[0])
                for o in range(KT):
                    wh, wl = (Wo[:, hh, l, o * P:(o + 1) * P] for l in range(2))
                    nc.tensor.matmul(bank[6 + o][:], wh, oT[:, 0, :], start=(hh == 0), stop=False)
                    nc.tensor.matmul(bank[6 + o][:], wh, oT[:, 1, :], start=False, stop=False)
                    ins = nc.tensor.matmul(bank[6 + o][:], wl, oT[:, 0, :], start=False, stop=(hh == HG - 1))
                ins.then_inc(s["y"], 1)

            it_now = [0]
            for jb in range(4):
                wait(pe, s["v_lo"], jb)
                v_block(jb, jb, 0)
            pe.wait_ge(s["v_lo"], 4)
            pe.wait_ge(s["wprep"], HG + 3)
            proj(Wq, 0, 0, 0, "q")
            proj(Wk, 1, 0, 0, "k")
            pe.wait_ge(s["q_lo"], 1)
            pe.wait_ge(s["k_lo"], 1)
            for qb in range(QB):
                scores(0, qb)

            def slot(j, c):
                u = 8 * j + c
                more = not last(j, c + 1)
                if more:
                    hh1 = (c + 1) % 4
                    tok = batch_of(j, c + 1) * S
                    pe.wait_ge(s["wprep"], group_of(j, c + 1) * PARTS_G + (HG + 3 * hh1 + 3))
                    wait(pe, s["v_lo"], min(u + 4, UNITS) if isinstance(u, int) else u + 4)
                    if isinstance(u, int) and (u == 0 or u > UNITS - 4):
                        pe.wait_ge(s["q_lo"], u + 1)
                    proj(Wq, 0, hh1, tok, "q")
                if not (isinstance(u, int) and u == 0):
                    it_now[0] = it_of(j, c - 1)
                    out_proj(u - 1, c - 1)
                pe.wait_ge(s["norm"], 4 * u + 4)
                trans(u, 0)
                if more:
                    wait(pe, s["o_lo"], u)
                    proj(Wk, 1, hh1, tok, "k")
                trans(u, 1)
                if not last(j, c + 4):
                    pe.wait_ge(s["q_lo"], u + 2)
                    v_block(u + 4, c % 4, it_of(j, c + 4))
                trans(u, 2)
                if more:
                    pe.wait_ge(s["q_lo"], u + 2)
                    pe.wait_ge(s["k_lo"], u + 2)
                    scores(u + 1, 0)
                trans(u, 3)
                pe.wait_ge(s["v_lo"], 4 * it_of(j, c) + 4)
                for qb in range(QB):
                    pv(u, qb, c)
                    if more and qb < QB - 1:
                        scores(u + 1, qb + 1)

            slots(pe, slot)
            out_proj(UNITS - 1, UNITS - 1)
            pe.wait_ge(s["y_add"], UNITS // 4)
            for i in range(NT):
                wait(pe, s["fin_add"], i - 1)
                for o in range(KT):
                    ins = nc.tensor.transpose(bank[i % 2][:, o * P:(o + 1) * P], yT[:, o, i * P:(i + 1) * P], ident)
                ins.then_inc(s["fin"], 1)


def _constants(np):
    c = np.zeros((P, C_N), np.float32)
    c[:, C_ID:C_ID + P] = np.eye(P)
    c[:, C_TRI:C_TRI + P] = np.triu(np.ones((P, P)), 1)
    c[:, C_ONE:C_ONE + P] = 1.0
    c[:, C_REV:C_REV + NE] = NE - np.arange(NE)
    c[:, C_J:C_J + NE] = P * np.arange(NE)
    c[:, C_LT:C_LT + NE * NE] = np.tril(np.ones((NE, NE)), -1).reshape(-1)
    c[:, C_I:C_I + NR] = np.arange(NR)
    return c


def kernel(**inputs):
    import numpy as np
    import concourse.bacc as bacc
    from concourse import mybir as _mybir
    from concourse.bass_utils import run_bass_kernel_spmd

    a = {k: np.asarray(v) for k, v in inputs.items()}
    f = {k[len("L0_ffn_"):]: v for k, v in a.items() if k.startswith("L0_ffn_")}
    w = {k[len("L0_attn_"):]: v for k, v in a.items() if k.startswith("L0_attn_")}

    def rows(x):
        return x.reshape(-1, P, x.shape[-1]).transpose(1, 0, 2)

    shared = [np.concatenate([rows(f["shared_gate_w"]), rows(f["shared_up_w"])], -1).reshape(P, -1),
              rows(f["shared_down_w"]).reshape(P, -1)]
    experts = [np.concatenate([np.concatenate([rows(f["gate_w"][e]), rows(f["up_w"][e])], -1).reshape(P, -1),
                               f["down_w"][e]], -1) for e in range(NE)]

    def part(kind, h):
        cd, sc = w[f"w{kind}_codes"], w[f"w{kind}_scales"]
        if kind == "o":
            return cd[h * P:(h + 1) * P], sc[4 * h:4 * h + 4]
        return (rows(cd[:, h * HD:(h + 1) * HD]).reshape(P, -1),
                sc[:, h * HD:(h + 1) * HD].reshape(KT, 4, HD).transpose(1, 0, 2).reshape(4, -1))

    order = [("v", HG * g + i) for g in range(NG) for i in range(HG)]
    parts = []
    for g in range(NG):
        parts += [part(*o) for o in order[HG * g:HG * g + HG]]
        parts += [part(k, HG * g + i) for i in range(HG) for k in "qko"]

    arrays = {
        "x": w["x"].reshape(NTOK, D),
        "consts": _constants(np),
        "router": rows(f["router_w"].T).reshape(P, -1),
        "ffn_w": np.concatenate(shared + experts, -1),
        "codes": np.stack([p[0] for p in parts]),
        "scales": np.stack([p[1] for p in parts]),
        "attn_bias": np.concatenate([w[k].reshape(H, HD).T for k in ("bq", "bk", "bv")], -1),
        "bo": w["bo"].reshape(KT, P).T,
    }
    arrays = {k: np.ascontiguousarray(v) for k, v in arrays.items()}
    nc = bacc.Bacc("TRN2", target_bir_lowering=False, num_devices=1)
    t = {k: nc.dram_tensor(f"in_{k}", v.shape, _mybir.dt.from_np(v.dtype), kind="ExternalInput").ap()
         for k, v in arrays.items()}
    t["out"] = nc.dram_tensor("out_x", (NTOK, D), _mybir.dt.float32, kind="ExternalOutput").ap()
    build(nc, t)
    r = run_bass_kernel_spmd(nc, [{f"in_{k}": v for k, v in arrays.items()}], core_ids=[0])
    return r.results[0]["out_x"].reshape(B, S, D)
```

```python
from contextlib import ExitStack

import concourse.bass as bass
from concourse import mybir

P = 128
F32 = mybir.dt.float32
F32R = mybir.dt.float32r
BF16 = mybir.dt.bfloat16
I32 = mybir.dt.int32
ALU = mybir.AluOpType
ACT = mybir.ActivationFunctionType
AX_X = mybir.AxisListType.X

B, S, D = 4, 512, 256
NTOK = B * S
NT = NTOK // P
KT = D // P
H, HD = 16, 128
QB = S // P
NE, TOPK, FE, FS = 16, 2, 128, 256
HG = 4
NG = H // HG
UNITS = B * H
LN_EPS = 1e-5
SM_SCALE = float(HD) ** -0.5

NSLOT_TILES = (NTOK * TOPK + NE * (P - 1)) // P
NR = -(-NSLOT_TILES // 4) * 4

CHUNK = 512
W_SH = KT * 2 * FS + (FS // P) * D
W_EX = KT * 2 * FE + D
W_ALL = W_SH + NE * W_EX
NCHUNK = W_ALL // CHUNK
SH_CHUNKS = W_SH // CHUNK
GR = 4
STEP_CHUNKS = (NCHUNK - SH_CHUNKS) // QB

PART = 2 * HD
PARTS_G = 4 * HG
NPARTS = NG * PARTS_G

C_ID, C_TRI, C_ONE, C_REV, C_J, C_LT, C_I = 0, 128, 256, 384, 400, 416, 672
C_POW = C_I + NR
C_N = C_POW + 8
VAR, RSTD, DELTA, HOT, TILES_KNOWN = 1, 2, 3, 4, 7


def wait(eng, sem, value):
    if isinstance(value, int) and value <= 0:
        return
    eng.wait_ge(sem, value)


class Carver:

    def __init__(self, tensor, start=0):
        self.t, self.at = tensor, start

    def cut(self, words):
        a = self.t[:, self.at:self.at + words]
        self.at += words
        return a


def build(nc, t):
    with ExitStack() as ctx:
        def sb(name, shape, dt=F32):
            return ctx.enter_context(nc.sbuf_tensor(name, shape, dt))

        m = {"ctx": ctx}
        m["X"] = sb("X", [P, NT, D])
        m["R"] = sb("R", [P, 37888], F32R)
        m["work"] = sb("work", [P, 8704])
        m["cst"] = sb("cst", [P, C_N])
        m["tri"] = sb("tri", [P, P], BF16)
        m["one"] = sb("one", [P, P], BF16)
        m["stats"] = sb("stats", [P, NT, 6])
        m["mv"] = sb("mv", [P, NT, 2])
        m["ln"] = sb("ln", [P, 5, NT])
        m["bank"] = [ctx.enter_context(nc.psum_tensor(f"bank{i}", [P, 512], F32)) for i in range(8)]
        m["xs_dram"] = nc.dram_tensor("xs_dram", (NR * P, D), F32, kind="Internal").ap()
        m["dn_dram"] = nc.dram_tensor("dn_dram", (NR * P, D), F32, kind="Internal").ap()
        ffn_phase(nc, t, m, 0)
        attention_phase(nc, t, m)
        ffn_phase(nc, t, m, 1)


def statistics_dve(nc, dve, m, s, x_ready, n):
    X, stats, mv, ln = m["X"], m["stats"], m["mv"], m["ln"]
    if x_ready is not None:
        dve.wait_ge(x_ready, 16)
    for i in range(NT):
        nc.vector.bn_stats(stats[:, i, :], X[:, i, :]).then_inc(s["ln"], 1)
    dve.wait_ge(s["ln"], n + NT)
    for i in range(NT):
        nc.vector.bn_aggr(mv[:, i, :], stats[:, i, :]).then_inc(s["ln"], 1)
    dve.wait_ge(s["ln"], n + 2 * NT)
    ve, sq, r, a, b = (ln[:, i, :] for i in range(5))
    nc.vector.tensor_scalar(ve, mv[:, :, 1], LN_EPS, None, ALU.add).then_inc(s["mark"], 1)
    dve.wait_ge(s["sqrt"], 1)
    n += 2 * NT
    for op in (lambda: nc.vector.reciprocal(r, sq),
               lambda: nc.vector.tensor_tensor(a, ve, r, ALU.mult),
               lambda: nc.vector.tensor_tensor(b, a, r, ALU.mult),
               lambda: nc.vector.tensor_scalar(a, b, -0.5, 1.5, ALU.mult, ALU.add),
               lambda: nc.vector.tensor_tensor(b, r, a, ALU.mult)):
        op().then_inc(s["ln"], 1)
        n += 1
        dve.wait_ge(s["ln"], n)
    nc.vector.scalar_tensor_tensor(out=a, in0=mv[:, :, 0], scalar=-1.0, in1=b, op0=ALU.mult, op1=ALU.mult)\
        .then_inc(s["mark"], 1)
    return n


def normalize_dve(nc, dve, m, xn, xT, s):
    X, mv, ln = m["X"], m["mv"], m["ln"]
    for q in range(QB + 1):
        if q < QB:
            for i in (4 * q, 4 * q + 1):
                nc.vector.tensor_scalar(xn[:, i, :], X[:, i, :], mv[:, i, 0:1], ln[:, 4, i:i + 1],
                                        ALU.subtract, ALU.mult).then_inc(s["xn"], 1)
        if q > 0:
            for kt in range(KT):
                n = (q - 1) * KT + kt
                dve.wait_ge(s["xt_hi"], n + 1)
                part = xT[:, :, kt, (q - 1) * S:q * S]
                nc.vector.tensor_tensor(part[:, 1], m["bank"][n % 2][:], part[:, 0].bitcast(F32), ALU.subtract)\
                    .then_inc(s["xt_lo"], 1)


def normalize_act(nc, act, m, xn, xT, s, after=None):
    X, ln = m["X"], m["ln"]
    act.wait_ge(s["mark"], VAR)
    nc.scalar.activation(ln[:, 1, :], ln[:, 0, :], ACT.Sqrt).then_inc(s["sqrt"], 1)
    act.wait_ge(s["mark"], RSTD)
    for q in range(QB + 1):
        if q < QB:
            for i in (4 * q + 2, 4 * q + 3):
                nc.scalar.activation(xn[:, i, :], X[:, i, :], ACT.Identity, bias=ln[:, 3, i:i + 1],
                                     scale=ln[:, 4, i:i + 1]).then_inc(s["xn_act"], 1)
        if q > 0:
            for kt in range(KT):
                n = (q - 1) * KT + kt
                act.wait_ge(s["xt"], n + 1)
                nc.scalar.activation(xT[:, 0, kt, (q - 1) * S:q * S], m["bank"][n % 2][:], ACT.Copy)\
                    .then_inc(s["xt_hi"], 1)
        if after is not None:
            after(q)


def transpose_pe(nc, pe, m, xn, s, after=None):
    ident = m["cst"][:, C_ID:C_ID + P]
    for q in range(QB):
        pe.wait_ge(s["xn"], 2 * q + 2)
        pe.wait_ge(s["xn_act"], 2 * q + 2)
        for kt in range(KT):
            n = q * KT + kt
            wait(pe, s["xt_lo"], n - 1)
            for i in range(4):
                last = nc.tensor.transpose(m["bank"][n % 2][:, i * P:(i + 1) * P],
                                           xn[:, 4 * q + i, kt * P:(kt + 1) * P], ident)
            last.then_inc(s["xt"], 1)
        if after is not None:
            after(q)


def product(nc, out, pairs):
    n = len(pairs)
    for i, (ah, al, bh, bl) in enumerate(pairs):
        nc.tensor.matmul(out, ah, bh, start=(i == 0), stop=False)
        nc.tensor.matmul(out, ah, bl, start=False, stop=False)
        last = nc.tensor.matmul(out, al, bh, start=False, stop=(i == n - 1))
    return last


def ffn_phase(nc, t, m, f):
    X, bank, cst = m["X"], m["bank"], m["cst"]
    xs_dram, dn_dram = m["xs_dram"], m["dn_dram"]
    r = Carver(m["R"])
    W = [r.cut(W_ALL), r.cut(W_ALL)]
    xT = r.cut(2 * KT * NTOK).rearrange("p (l k n) -> p l k n", l=2, k=KT)
    small = r.at
    hT = r.cut(2 * 2 * S).rearrange("p (j l n) -> p j l n", j=2, l=2)
    r = Carver(m["R"], small)
    xsT = r.cut(2 * 2 * KT * P).rearrange("p (b l k n) -> p b l k n", b=2, l=2, k=KT)
    hrT = r.cut(2 * 2 * P).rearrange("p (b l n) -> p b l n", b=2, l=2)
    w = Carver(m["work"])
    xn = w.cut(NT * D).rearrange("p (t d) -> p t d", t=NT)
    stage = w.cut(4 * CHUNK)
    stg = stage.rearrange("p (b n) -> p b n", b=4)
    dnb = stage[:, 0:4 * D].rearrange("p (b d) -> p b d", b=4)
    small = w.at
    sg = w.cut(2 * S).rearrange("p (j n) -> p j n", j=2)
    hf = w.cut(S)
    w = Carver(m["work"], small)
    xs = w.cut(4 * D).rearrange("p (b d) -> p b d", b=4)
    sgr = w.cut(2 * P).rearrange("p (b n) -> p b n", b=2)
    hr = w.cut(2 * P).rearrange("p (b n) -> p b n", b=2)
    G = m["work"][:, small:small + GR * D].rearrange("p (b d) -> p b d", b=GR)
    te3 = lambda a: a.rearrange("p (t e) -> p t e", t=NT)
    lgT = m["work"][0:NE, small:small + 2 * S].rearrange("e (b n) -> e b n", b=2)
    route = w.cut(4 * 256)
    L, oh1, oh2, tmp = (te3(route[:, i * 256:(i + 1) * 256]) for i in range(4))
    zero = route[:, 512:512 + D]
    tec = route[0:1, 0:NR * NE].rearrange("p (i e) -> p i e", e=NE)

    with ExitStack() as ctx:
        sems = {}

        def sem(name):
            sems[name] = m["ctx"].enter_context(nc.semaphore(f"f{f}_{name}"))
            return sems[name]

        def sb(name, shape, dt=F32):
            return ctx.enter_context(nc.sbuf_tensor(f"f{f}_{name}", shape, dt))

        A = sb("A", [P, NT + 1, NE], BF16)
        rt = sb("rt", [P, 8, NT])
        pos = [sb(f"pos{k}", [P, NT], I32) for k in range(TOPK)]
        wt = [sb(f"wt{k}", [P, NT]) for k in range(TOPK)]
        rwT = sb("rwT", [P, KT, NE])
        rw = sb("rw", [P, 2, KT, NE], F32R)
        ex = sb("ex", [P, 4, NE])
        tef = sb("tef", [1, NR + 8])
        tep = sb("tep", [1, 2, NR + 4])
        pk = sb("pk", [1, 2, NR // 4 + 1])
        packed = sb("packed", [1, NR // 4 + 1], I32)
        s = sems
        for name in ("x_in", "cst_in", "rw_in", "zeroed", "zfill", "tri", "ln", "mark", "sqrt", "xn", "xn_act", "xt",
                     "xt_hi", "xt_lo", "rw", "lgT", "lg_sb", "logit", "rank",
                     "w_hi", "w_lo", "gu", "silu", "h", "h_hi", "h_lo", "dn", "x_add",
                     "scat", "r_xt", "r_xhi", "r_xlo", "r_gu", "r_silu", "r_h", "r_ht", "r_hhi", "r_hlo",
                     "r_dn", "r_ev0", "r_ev1", "comb"):
            if f == 0 or name not in ("x_in", "cst_in", "zeroed", "zfill", "tri"):
                sem(name)
        w_in = [sem(f"w_in{i}") for i in range(4)]
        xs_in = [sem(f"xs_in{i}") for i in range(2)]
        dn_out = [sem(f"dn_out{i}") for i in range(4)]
        g_in = [sem(f"g_in{i}") for i in range(GR)]
        if f == 1:
            sem("out")
        block = ctx.enter_context(nc.Block())

        ident = cst[:, C_ID:C_ID + P]

        def slots(eng, slot):
            for c in range(-1, 8):
                slot(0, c)
            with eng.Fori(2, NR // 4 - 1) as j:
                for c in range(4):
                    slot(j, c)
            for c in range(NR - 4, NR + 2):
                slot(0, c)

        def tiles(eng, do):
            for c in range(4):
                do(0, c)
            with eng.Fori(1, NR // 4) as j:
                for c in range(4):
                    do(j, c)

        def live(j, c):
            return not isinstance(j, int) or 0 <= 4 * j + c < NR

        def evac_dn(ns, eng, j, c):
            n = 4 * j + c
            eng.wait_ge(s["r_dn"], n + 1)
            wait(eng, dn_out[c % 4], 16 * (j + c // 4))
            if ns is nc.scalar:
                ins = nc.scalar.activation(dnb[:, c % 4, :], bank[6 + c % 2][:, 0:D], ACT.Copy)
            else:
                ins = nc.vector.tensor_copy(dnb[:, c % 4, :], bank[6 + c % 2][:, 0:D])
            ins.then_inc(s[f"r_ev{c % 2}"], 1)

        @block.sync
        def _(sp):
            if f == 0:
                sp.dma_start(X[:], t["x"].rearrange("(t p) d -> p t d", p=P)).then_inc(s["x_in"], 16)
                sp.dma_start(cst[:], t["consts"]).then_inc(s["cst_in"], 16)
            sp.dma_start(rwT[:], t["router"].rearrange("p (k e) -> p k e", k=KT)).then_inc(s["rw_in"], 16)

            def chunk(c, b):
                wait(sp, s["w_lo"], c - 3)
                sp.dma_start(stg[:, b, :], t["ffn_w"][:, bass.ds(c * CHUNK, CHUNK)]).then_inc(w_in[b], 16)

            for c in range(4):
                chunk(c, c)
            if f == 0:
                sp.wait_ge(s["zeroed"], 1)
                sp.dma_start(xs_dram.rearrange("(p n) d -> p n d", p=P),
                             zero.unsqueeze(1).broadcast_to([P, NR, D])).then_inc(s["zfill"], 16)
            with sp.Fori(1, NCHUNK // 4) as j:
                for b in range(4):
                    chunk(j * 4 + b, b)
            for c in range(NCHUNK // 4 * 4, NCHUNK):
                chunk(c, c % 4)

            sp.wait_ge(s["scat"], 16 * NT * TOPK)
            sp.wait_ge(s["x_add"], NT)

            def load(j, c):
                i = 4 * j + c
                wait(sp, s["r_xt"], i - 2)
                sp.dma_start(xs[:, c % 4:c % 4 + 2, :],
                             xs_dram[bass.ds(i * P, 2 * P), :].rearrange("(t p) d -> p t d", p=P))\
                    .then_inc(xs_in[c % 4 // 2], 16)

            def store(j, c):
                n = 4 * j + c
                sp.wait_ge(s[f"r_ev{c % 2}"], 2 * j + (c // 2 + 1))
                sp.dma_start(dn_dram[bass.ds(n * P, P), :], dnb[:, c % 4, :]).then_inc(dn_out[c % 4], 16)

            load(0, 0)
            load(0, 2)
            for c in range(4):
                if c % 2 == 0:
                    load(0, c + 4)
                if c == 3:
                    store(0, 0)
            with sp.Fori(1, NR // 4 - 1) as j:
                for c in range(4):
                    if c % 2 == 0:
                        load(j, c + 4)
                    store(j, c - 3)
            for n in range(NR - 7, NR):
                store(0, n)
            if f == 1:
                out_v = t["out"].rearrange("(t p) d -> p t d", p=P)
                for q in range(QB):
                    sp.wait_ge(s["comb"], TOPK * 4 * (q + 1))
                    sp.dma_start(out_v[:, 4 * q:4 * q + 4, :], X[:, 4 * q:4 * q + 4, :]).then_inc(s["out"], 16)
                sp.wait_ge(s["out"], 16 * QB)

        @block.gpsimd
        def _(pool):
            if f == 0:
                nc.gpsimd.memset(zero, 0.0).then_inc(s["zeroed"], 1)
                pool.wait_ge(s["zfill"], 16)
            for i in range(NT):
                for k in range(TOPK):
                    if i == 0:
                        pool.wait_ge(s["mark"], HOT + 1 + k)
                    if i == 0 and k == 0:
                        pool.wait_ge(s["xn"], NT // 2)
                        pool.wait_ge(s["xn_act"], NT // 2)
                    nc.gpsimd.indirect_dma_start(
                        out=xs_dram, out_offset=bass.IndirectOffsetOnAxis(ap=pos[k][:, i:i + 1], axis=0),
                        in_=xn[:, i, :], in_offset=None).then_inc(s["scat"], 16)
            for i in range(4):
                pool.wait_ge(dn_out[i], 16 * (NR // 4))
            pool.wait_ge(s["r_ev0"], NR // 2)
            pool.wait_ge(s["r_ev1"], NR // 2)
            for n in range(NT * TOPK):
                i, k = divmod(n, TOPK)
                wait(pool, s["comb"], n - GR + 1)
                nc.gpsimd.indirect_dma_start(
                    out=G[:, n % GR, :], out_offset=None, in_=dn_dram,
                    in_offset=bass.IndirectOffsetOnAxis(ap=pos[k][:, i:i + 1], axis=0)).then_inc(g_in[n % GR], 16)

        @block.scalar
        def _(act):
            act.wait_ge(s["rw_in"], 16)
            nc.scalar.activation(rw[:, 0], rwT[:], ACT.Copy).then_inc(s["rw"], 1)

            def logits_out(q):
                if q >= 1:
                    act.wait_ge(s["lgT"], q)
                    wait(act, s["logit"], q - 2)
                    nc.scalar.activation(lgT[:, (q - 1) % 2, :], bank[2 + 4 * ((q - 1) % 2)][0:NE, :], ACT.Copy)\
                        .then_inc(s["lg_sb"], 1)

            normalize_act(nc, act, m, xn, xT, s, logits_out)

            def split_hi(c, q, b):
                act.wait_ge(w_in[b], q * 16 + 16)
                nc.scalar.activation(W[0][:, bass.ds(c * CHUNK, CHUNK)], stg[:, b, :], ACT.Copy)\
                    .then_inc(s["w_hi"], 1)

            for c in range(SH_CHUNKS):
                split_hi(c, c // 4, c % 4)
            act.wait_ge(s["mark"], DELTA)
            nc.scalar.activation(rt[:, 5, :], rt[:, 4, :], ACT.Exp).then_inc(s["sqrt"], 1)

            def shared(pair, half):
                step = pair * 2 + half
                for j in range(2):
                    k = step * 2 + j
                    act.wait_ge(s["gu"], k + 1)
                    wait(act, s["h"], k - 1)
                    nc.scalar.activation(sg[:, j, :], bank[j][:], ACT.Silu).then_inc(s["silu"], 1)
                    act.wait_ge(s["h"], k + 1)
                    wait(act, s["dn"], step * 4)
                    nc.scalar.activation(hT[:, j, 0, :], hf, ACT.Copy).then_inc(s["h_hi"], 1)
                for c in range(STEP_CHUNKS):
                    n = SH_CHUNKS + half * STEP_CHUNKS + c
                    split_hi(pair * 2 * STEP_CHUNKS + n, pair * (2 * STEP_CHUNKS // 4) + n // 4, n % 4)

            shared(0, 0)
            shared(0, 1)
            shared(1, 0)
            shared(1, 1)
            act.wait_ge(s["x_add"], NT)

            def slot(j, c):
                i = 4 * j + c
                if live(j, c + 1):
                    act.wait_ge(s["r_xt"], i + 2)
                    wait(act, s["r_gu"], i)
                    nc.scalar.activation(xsT[:, (c + 1) % 2, 0].rearrange("p k n -> p (k n)"),
                                         bank[(c + 1) % 2][:, 0:D], ACT.Copy).then_inc(s["r_xhi"], 1)
                if live(j, c):
                    act.wait_ge(s["r_gu"], i + 1)
                    wait(act, s["r_h"], i - 1)
                    nc.scalar.activation(sgr[:, c % 2, :], bank[2 + c % 2][:, 0:FE], ACT.Silu)\
                        .then_inc(s["r_silu"], 1)
                if live(j, c - 1):
                    act.wait_ge(s["r_ht"], i)
                    wait(act, s["r_dn"], i - 2)
                    nc.scalar.activation(hrT[:, (c - 1) % 2, 0, :], bank[4 + (c - 1) % 2][:, 0:P], ACT.Copy)\
                        .then_inc(s["r_hhi"], 1)
                if live(j, c - 2) and c % 2 == 0:
                    evac_dn(nc.scalar, act, j, c - 2)

            slots(act, slot)

        @block.vector
        def _(dve):
            if f == 0:
                dve.wait_ge(s["cst_in"], 16)
                nc.vector.tensor_copy(m["tri"][:], cst[:, C_TRI:C_TRI + P])
                nc.vector.tensor_copy(m["one"][:], cst[:, C_ONE:C_ONE + P]).then_inc(s["tri"], 1)
            nc.vector.memset(A[:, 0, :], 0.0)
            nc.vector.memset(tef[:], 0.0).then_inc(s["ln"], 1)
            ln_steps = statistics_dve(nc, dve, m, s, s["x_in"] if f == 0 else None, 1)
            dve.wait_ge(s["rw"], 1)
            nc.vector.tensor_tensor(rw[:, 1], rwT[:], rw[:, 0].bitcast(F32), ALU.subtract).then_inc(s["rw"], 1)
            normalize_dve(nc, dve, m, xn, xT, s)

            def split_lo(c, b):
                dve.wait_ge(s["w_hi"], c + 1)
                nc.vector.tensor_tensor(W[1][:, bass.ds(c * CHUNK, CHUNK)], stg[:, b, :],
                                        W[0][:, bass.ds(c * CHUNK, CHUNK)].bitcast(F32), ALU.subtract)\
                    .then_inc(s["w_lo"], 1)

            for c in range(SH_CHUNKS):
                split_lo(c, c % 4)

            n = [ln_steps]

            def link(ins):
                ins.then_inc(s["ln"], 1)
                n[0] += 1
                dve.wait_ge(s["ln"], n[0])

            rev = cst[:, C_REV:C_REV + NE].unsqueeze(1).broadcast_to([P, NT, NE])
            m1, r1, m2, r2, dl, e2, w1 = (rt[:, i, :] for i in range(7))
            wide = lambda a: a.unsqueeze(2).broadcast_to([P, NT, NE])
            dve.wait_ge(s["logit"], QB)
            if f == 0:
                dve.wait_ge(s["zfill"], 16)
            link(nc.vector.tensor_copy(L, te3(bank[3][:, 0:256])))
            link(nc.vector.reduce_max(m1, L, AX_X))
            link(nc.vector.tensor_tensor(tmp, L, wide(m1), ALU.is_equal))
            link(nc.vector.tensor_tensor(tmp, tmp, rev, ALU.mult))
            link(nc.vector.reduce_max(r1, tmp, AX_X))
            link(nc.vector.tensor_tensor(oh1, rev, wide(r1), ALU.is_equal))
            link(nc.vector.scalar_tensor_tensor(out=L, in0=oh1, scalar=-3.0e38, in1=L, op0=ALU.mult, op1=ALU.add))
            link(nc.vector.reduce_max(m2, L, AX_X))
            nc.vector.tensor_tensor(dl, m2, m1, ALU.subtract).then_inc(s["mark"], 1)
            link(nc.vector.tensor_tensor(tmp, L, wide(m2), ALU.is_equal))
            link(nc.vector.tensor_tensor(tmp, tmp, rev, ALU.mult))
            link(nc.vector.reduce_max(r2, tmp, AX_X))
            link(nc.vector.tensor_tensor(oh2, rev, wide(r2), ALU.is_equal))
            nc.vector.tensor_tensor(A[:, 1:, :], oh1, oh2, ALU.add).then_inc(s["mark"], 1)
            dve.wait_ge(s["sqrt"], 2)
            link(nc.vector.tensor_scalar(w1, e2, 1.0, None, ALU.add))
            link(nc.vector.reciprocal(r1, w1))
            link(nc.vector.tensor_scalar(wt[0][:], r1, 0.5, None, ALU.mult))
            link(nc.vector.tensor_tensor(wt[1][:], wt[0][:], e2, ALU.mult))
            dve.wait_ge(s["rank"], 1)
            cnt = ex[:, 0, :]
            link(nc.vector.tensor_copy(cnt, bank[3][:, 256:256 + NE]))
            jj = cst[:, C_J:C_J + NE].unsqueeze(1).broadcast_to([P, NE, NE])
            lt = cst[:, C_LT:C_LT + NE * NE].rearrange("p (a b) -> p a b", a=NE)
            link(nc.vector.tensor_tensor(tmp, cnt.unsqueeze(2).broadcast_to([P, NE, NE]), jj, ALU.is_gt))
            link(nc.vector.reduce_sum(ex[:, 1, :], tmp, AX_X))
            link(nc.vector.tensor_tensor(tmp, ex[:, 1, :].unsqueeze(1).broadcast_to([P, NE, NE]), lt, ALU.mult))
            link(nc.vector.reduce_sum(ex[:, 2, :], tmp, AX_X))
            link(nc.vector.tensor_scalar(ex[:, 3, :], ex[:, 2, :], float(P), None, ALU.mult))
            link(nc.vector.tensor_tensor(tmp, te3(bank[3][:, 0:256]),
                                         ex[:, 3, :].unsqueeze(1).broadcast_to([P, NT, NE]), ALU.add))
            for k, oh in enumerate((oh1, oh2)):
                link(nc.vector.tensor_tensor(oh, oh, tmp, ALU.mult))
                link(nc.vector.reduce_sum(rt[:, k, :], oh, AX_X))
                nc.vector.tensor_copy(pos[k][:], rt[:, k, :]).then_inc(s["mark"], 1)
            link(nc.vector.tensor_tensor(ex[:, 0, :], ex[:, 1, :], ex[:, 2, :], ALU.add))
            link(nc.vector.tensor_tensor(tec, ex[0:1, 0, :].unsqueeze(1).broadcast_to([1, NR, NE]),
                                         cst[0:1, C_I:C_I + NR].unsqueeze(2).broadcast_to([1, NR, NE]), ALU.is_le))
            link(nc.vector.reduce_sum(tef[:, 2:2 + NR], tec, AX_X))
            link(nc.vector.tensor_scalar(tef[:, 2:2 + NR], tef[:, 2:2 + NR], float(NE - 1), None, ALU.min))
            four = lambda a: a.rearrange("p (j c) -> p j c", c=4)
            pw = cst[0:1, C_POW:C_POW + 8].unsqueeze(1).broadcast_to([1, NR // 4 + 1, 8])
            nc.vector.tensor_tensor(four(tep[:, 0, :]), four(tef[:, 2:2 + NR + 4]), pw[:, :, 0:4], ALU.mult)
            link(nc.vector.tensor_tensor(four(tep[:, 1, :]), four(tef[:, 0:NR + 4]), pw[:, :, 4:8], ALU.mult))
            link(nc.vector.reduce_sum(pk[:], tep[:].rearrange("p a (j c) -> p a j c", c=4), AX_X))
            nc.vector.tensor_tensor(packed[:], pk[:, 0, :], pk[:, 1, :], ALU.add).then_inc(s["mark"], 1)

            def shared(pair, half):
                step = pair * 2 + half
                for j in range(2):
                    k = step * 2 + j
                    dve.wait_ge(s["silu"], k + 1)
                    wait(dve, s["h_lo"], k)
                    nc.vector.tensor_tensor(hf, bank[4 + j][:], sg[:, j, :], ALU.mult).then_inc(s["h"], 1)
                    dve.wait_ge(s["h_hi"], k + 1)
                    nc.vector.tensor_tensor(hT[:, j, 1, :], hf, hT[:, j, 0, :].bitcast(F32), ALU.subtract)\
                        .then_inc(s["h_lo"], 1)
                for q in range(QB):
                    dve.wait_ge(s["dn"], step * 4 + (q + 1))
                    xi = X[:, bass.ds(step * 4 + q, 1), :].rearrange("p a d -> p (a d)")
                    nc.vector.scalar_tensor_tensor(out=xi, in0=bank[6 + q % 2][:, 0:D], scalar=0.5, in1=xi,
                                                   op0=ALU.mult, op1=ALU.add).then_inc(s["x_add"], 1)
                for c in range(STEP_CHUNKS):
                    n = SH_CHUNKS + half * STEP_CHUNKS + c
                    split_lo(pair * 2 * STEP_CHUNKS + n, n % 4)

            shared(0, 0)
            shared(0, 1)
            shared(1, 0)
            shared(1, 1)

            def slot(j, c):
                i = 4 * j + c
                if live(j, c + 1):
                    dve.wait_ge(s["r_xhi"], i + 2)
                    nc.vector.tensor_tensor(xsT[:, (c + 1) % 2, 1].rearrange("p k n -> p (k n)"),
                                            bank[(c + 1) % 2][:, 0:D],
                                            xsT[:, (c + 1) % 2, 0].rearrange("p k n -> p (k n)").bitcast(F32),
                                            ALU.subtract).then_inc(s["r_xlo"], 1)
                if live(j, c):
                    dve.wait_ge(s["r_silu"], i + 1)
                    wait(dve, s["r_ht"], i - 1)
                    nc.vector.tensor_tensor(hr[:, c % 2, :], bank[2 + c % 2][:, FE:2 * FE], sgr[:, c % 2, :],
                                            ALU.mult).then_inc(s["r_h"], 1)
                if live(j, c - 1):
                    dve.wait_ge(s["r_hhi"], i)
                    nc.vector.tensor_tensor(hrT[:, (c - 1) % 2, 1, :], bank[4 + (c - 1) % 2][:, 0:P],
                                            hrT[:, (c - 1) % 2, 0, :].bitcast(F32), ALU.subtract)\
                        .then_inc(s["r_hlo"], 1)
                if live(j, c - 2) and c % 2 == 1:
                    evac_dn(nc.vector, dve, j, c - 2)

            slots(dve, slot)
            for k in range(NT * TOPK):
                i, kk = divmod(k, TOPK)
                dve.wait_ge(g_in[k % GR], 16 * (k // GR + 1))
                wait(dve, s["comb"], k)
                nc.vector.scalar_tensor_tensor(out=X[:, i, :], in0=G[:, k % GR, :], scalar=wt[kk][:, i:i + 1],
                                               in1=X[:, i, :], op0=ALU.mult, op1=ALU.add).then_inc(s["comb"], 1)

        @block.tensor
        def _(pe):
            if f == 0:
                pe.wait_ge(s["cst_in"], 16)

            def logits(q):
                if q == 0:
                    pe.wait_ge(s["rw"], 2)
                pe.wait_ge(s["xt_lo"], KT * q + KT)
                wait(pe, s["lg_sb"], q - 1)
                product(nc, bank[2 + 4 * (q % 2)][0:NE, :],
                        [(rw[:, 0, kt, :], rw[:, 1, kt, :], xT[:, 0, kt, q * S:(q + 1) * S],
                          xT[:, 1, kt, q * S:(q + 1) * S]) for kt in range(KT)]).then_inc(s["lgT"], 1)

            def logits_back(q):
                pe.wait_ge(s["lg_sb"], q + 1)
                for i in range(4):
                    n = 4 * q + i
                    last = nc.tensor.transpose(bank[3][:, n * NE:(n + 1) * NE], lgT[:, q % 2, i * P:(i + 1) * P],
                                               ident[0:NE, 0:NE])
                last.then_inc(s["logit"], 1)

            def behind(q):
                if q >= 1:
                    logits(q - 1)
                if q >= 2:
                    logits_back(q - 2)

            transpose_pe(nc, pe, m, xn, s, behind)
            logits(QB - 1)
            logits_back(QB - 2)
            logits_back(QB - 1)

            wv = [w_[:, 0:W_SH - 2 * D].rearrange("p (k g n) -> p k g n", k=KT, g=2) for w_ in W]
            wd = [w_[:, W_SH - 2 * D:W_SH].rearrange("p (j n) -> p j n", j=2) for w_ in W]

            def gate_up(step, j):
                k = step * 2 + j
                wait(pe, s["h"], k - 1)
                for g, out in ((0, bank[j]), (1, bank[4 + j])):
                    last = product(nc, out[:], [(wv[0][:, kt, g, j * P:(j + 1) * P], wv[1][:, kt, g, j * P:(j + 1) * P],
                                                 xT[:, 0, kt, bass.ds(step * S, S)],
                                                 xT[:, 1, kt, bass.ds(step * S, S)]) for kt in range(KT)])
                last.then_inc(s["gu"], 1)

            def down(step):
                pe.wait_ge(s["h_lo"], step * 2 + 2)
                for q in range(QB):
                    wait(pe, s["x_add"], step * 4 + (q - 1))
                    product(nc, bank[6 + q % 2][:, 0:D],
                            [(hT[:, j, 0, q * P:(q + 1) * P], hT[:, j, 1, q * P:(q + 1) * P],
                              wd[0][:, j, :], wd[1][:, j, :]) for j in range(2)]).then_inc(s["dn"], 1)

            pe.wait_ge(s["w_lo"], SH_CHUNKS)
            gate_up(0, 0)
            gate_up(0, 1)
            if f == 0:
                pe.wait_ge(s["tri"], 1)
            pe.wait_ge(s["mark"], HOT)
            flatA = A[:].rearrange("p t e -> p (t e)")
            nc.tensor.matmul(bank[3][:, 0:256], m["tri"][:], flatA[:, NE:], start=True, stop=False)
            for back in range(NT - 1, 1, -1):
                nc.tensor.matmul(bank[3][:, back * NE:256], m["one"][:], flatA[:, NE:NE + 256 - back * NE],
                                 start=False, stop=False)
            nc.tensor.matmul(bank[3][:, 0:256], m["one"][:], flatA[:, 0:256], start=False, stop=True)
            for i in range(NT):
                last = nc.tensor.matmul(bank[3][:, 256:256 + NE], m["one"][:], A[:, i + 1, :],
                                        start=(i == 0), stop=(i == NT - 1))
            last.then_inc(s["rank"], 1)
            gate_up(1, 0)
            down(0)
            with pe.Fori(1, QB - 1) as step:
                gate_up(step, 1)
                gate_up(step + 1, 0)
                down(step)
            gate_up(QB - 1, 1)
            down(QB - 1)

            pe.wait_ge(s["w_lo"], NCHUNK)
            pe.wait_ge(s["mark"], TILES_KNOWN)
            we = [w_[:, W_SH:W_ALL].rearrange("p (e n) -> p e n", e=NE) for w_ in W]

            word = [None]

            def slot(j, c):
                i = 4 * j + c
                if c % 4 == 0:
                    word[0] = pe.value_load(packed[0:1, bass.ds(j + c // 4, 1)], min_val=0, max_val=(1 << 24) - 1)

                def expert(place):
                    return (word[0] >> (4 * place)) & (NE - 1)

                if live(j, c + 1):
                    b = (c + 1) % 2
                    if b == 0:
                        pe.wait_ge(xs_in[(c + 1) % 4 // 2], 16 * (j + (c + 1) // 4) + 16)
                    wait(pe, s["r_xlo"], i)
                    for kt in range(KT):
                        last = nc.tensor.transpose(bank[b][:, kt * P:(kt + 1) * P],
                                                   xs[:, (c + 1) % 4, kt * P:(kt + 1) * P], ident)
                    last.then_inc(s["r_xt"], 1)
                if live(j, c):
                    b = c % 2
                    e = expert(c % 4)
                    pe.wait_ge(s["r_xlo"], i + 1)
                    wait(pe, s["r_h"], i - 1)
                    gu = [[w_[:, bass.ds(e, 1), kt * 2 * FE:(kt + 1) * 2 * FE].rearrange("p a n -> p (a n)")
                           for w_ in we] for kt in range(KT)]
                    product(nc, bank[2 + b][:, 0:2 * FE],
                            [(xsT[:, b, 0, kt, :], xsT[:, b, 1, kt, :], gu[kt][0], gu[kt][1])
                             for kt in range(KT)]).then_inc(s["r_gu"], 1)
                if live(j, c - 1):
                    b = (c - 1) % 2
                    pe.wait_ge(s["r_h"], i)
                    wait(pe, s["r_hlo"], i - 2)
                    nc.tensor.transpose(bank[4 + b][:, 0:P], hr[:, b, :], ident).then_inc(s["r_ht"], 1)
                if live(j, c - 2):
                    b = c % 2
                    e = expert(c % 4 + 4 if c % 4 < 2 else c % 4 - 2)
                    pe.wait_ge(s["r_hlo"], i - 1)
                    wait(pe, s[f"r_ev{b}"], 2 * j + (c - 2) // 2)
                    d = [w_[:, bass.ds(e, 1), KT * 2 * FE:W_EX].rearrange("p a n -> p (a n)") for w_ in we]
                    product(nc, bank[6 + b][:, 0:D], [(hrT[:, b, 0, :], hrT[:, b, 1, :], d[0], d[1])])\
                        .then_inc(s["r_dn"], 1)

            slots(pe, slot)


def attention_phase(nc, t, m):
    X, bank, cst = m["X"], m["bank"], m["cst"]
    r = Carver(m["R"])
    xT = r.cut(2 * KT * NTOK).rearrange("p (l k n) -> p l k n", l=2, k=KT)
    vx = r.cut(4 * 2 * KT * P).rearrange("p (j l k n) -> p j l k n", j=4, l=2, k=KT)
    Wq, Wk, Wo = (r.cut(HG * 2 * PART).rearrange("p (h l n) -> p h l n", h=HG, l=2) for _ in range(3))
    Wv = r.cut(2 * 2 * KT * HG * HD).rearrange("p (g l k n) -> p g l k n", g=2, l=2, k=KT)
    V = r.cut(2 * 2 * QB * HG * HD).rearrange("p (i l b n) -> p i l b n", i=2, l=2, b=QB)
    qT = r.cut(2 * S).rearrange("p (l n) -> p l n", l=2)
    kT = r.cut(2 * S).rearrange("p (l n) -> p l n", l=2)
    PT = r.cut(2 * QB * S).rearrange("p (l b n) -> p l b n", l=2, b=QB)
    oT = r.cut(2 * S).rearrange("p (l n) -> p l n", l=2)
    assert r.at <= 37888
    w = Carver(m["work"])
    flat = w.cut(NT * D)
    xn = flat.rearrange("p (t d) -> p t d", t=NT)
    yT = flat.rearrange("p (o n) -> p o n", o=KT)
    Pm = w.cut(QB * S).rearrange("p (q n) -> p q n", q=QB)
    raw = w.cut(2 * 4 * PART).rearrange("p (c b n) -> p c b n", c=2, b=4)

    with ExitStack() as ctx:
        s = {}

        def sem(name):
            s[name] = m["ctx"].enter_context(nc.semaphore(f"a_{name}"))
            return s[name]

        def sb(name, shape, dt=F32):
            return ctx.enter_context(nc.sbuf_tensor(f"a_{name}", shape, dt))

        bias = sb("bias", [P, 3, H])
        bslot = sb("bslot", [P, HG, 3])
        bo = sb("bo", [P, KT])
        mx = sb("mx", [P, QB])
        sm = sb("sm", [P, QB])
        ri = sb("ri", [P, QB])
        for name in ("b_in", "ln", "mark", "sqrt", "xn", "xn_act", "xt", "xt_hi", "xt_lo", "wstep", "wprep",
                     "q", "k", "v", "s", "t", "o", "y", "q_hi", "q_lo", "k_hi", "k_lo", "v_hi", "v_lo",
                     "max", "exp", "rsum", "norm", "norm_act", "t_hi", "t_lo", "o_hi", "o_lo", "y_add", "fin", "fin_add"):
            sem(name)
        raw_in = [sem(f"raw_in{i}") for i in range(4)]
        vx_in = [sem(f"vx_in{i}") for i in range(4)]
        block = ctx.enter_context(nc.Block())
        ident = cst[:, C_ID:C_ID + P]

        LOOP0, LOOP1 = 1, UNITS // 8 - 1

        def slots(eng, slot):
            for c in range(8 * LOOP0):
                slot(0, c)
            with eng.Fori(LOOP0, LOOP1) as j:
                for c in range(8):
                    slot(j, c)
            for c in range(8 * LOOP1, UNITS):
                slot(0, c)

        def it_of(j, c):
            return 2 * j + c // 4

        def batch_of(j, c):
            return it_of(j, c) % B

        def group_of(j, c):
            return it_of(j, c) // B

        def last(j, c):
            return isinstance(j, int) and 8 * j + c >= UNITS

        def load_vx(eng, n_it, jb, n):
            wait(eng, s["v"], n - 3)
            eng.dma_start(vx[:, jb].bitcast(F32).rearrange("p l k n -> p (l k) n"),
                          xT[:, :, :, bass.ds((n_it % B) * S + jb * P, P)].bitcast(F32)
                          .rearrange("p l k n -> p (l k) n")).then_inc(vx_in[jb], 16)

        @block.sync
        def _(sp):
            sp.dma_start(bias[:], t["attn_bias"].rearrange("p (a h) -> p a h", a=3)).then_inc(s["b_in"], 16)
            sp.dma_start(bo[:], t["bo"]).then_inc(s["b_in"], 16)

            def part(j, b):
                n = 4 * j + b
                wait(sp, s["wprep"], n - 3)
                sp.dma_start(raw[:, 0, b, :], t["codes"][bass.ds(n, 1), :, :].rearrange("a p n -> (a p) n"))\
                    .then_inc(raw_in[b], 16)
                for k in range(4):
                    sp.dma_start(raw[32 * k:32 * k + 32, 1, b, :],
                                 t["scales"][bass.ds(n, 1), k, :].broadcast_to([32, PART]))\
                        .then_inc(raw_in[b], 16)

            for b in range(4):
                part(0, b)
            with sp.Fori(1, NPARTS // 4) as j:
                for b in range(4):
                    part(j, b)

        @block.gpsimd
        def _(pool):
            pool.wait_ge(s["b_in"], 32)
            steps = [0]

            def link(ins):
                steps[0] += 1
                ins.then_inc(s["wstep"], 1)
                pool.wait_ge(s["wstep"], steps[0])

            link(nc.gpsimd.tensor_scalar(bias[:, 0, :], bias[:, 0, :], SM_SCALE, None, ALU.mult))
            n = 0
            for g in range(NG):
                for kind, hh in [("v", i) for i in range(HG)] + [(k, i) for i in range(HG) for k in "qko"]:
                    pool.wait_ge(raw_in[n % 4], 80 * (n // 4 + 1))
                    codes, scales = raw[:, 0, n % 4, :], raw[:, 1, n % 4, :]
                    if kind == "q":
                        link(nc.gpsimd.tensor_scalar(scales, scales, SM_SCALE, None, ALU.mult))
                    link(nc.gpsimd.tensor_tensor(codes, codes, scales, ALU.mult))
                    if kind == "v":
                        wait(pool, s["v"], 16 * g - 16)
                        hi, lo = (Wv[:, g % 2, l, :, hh * HD:(hh + 1) * HD] for l in range(2))
                        src = codes.rearrange("p (k n) -> p k n", k=KT)
                    else:
                        slot = {"q": Wq, "k": Wk, "o": Wo}[kind]
                        hi, lo = slot[:, hh, 0, :], slot[:, hh, 1, :]
                        src = codes
                        if kind in "qk":
                            wait(pool, s["k_lo"], 16 * g - 3 + hh)
                            if kind == "q" and g > 0:
                                pool.wait_ge(s["y"], 16 * g - 3 + hh)
                        else:
                            wait(pool, s["y"], 16 * g - 3 + hh)
                    if kind == "q":
                        link(nc.gpsimd.tensor_copy(bslot[:, hh, :], bias[:, :, 4 * g + hh]))
                    link(nc.gpsimd.tensor_copy(hi, src))
                    nc.gpsimd.tensor_tensor(lo, src, hi.bitcast(F32), ALU.subtract).then_inc(s["wprep"], 1)
                    n += 1

        @block.scalar
        def _(act):
            normalize_act(nc, act, m, xn, xT, s)
            act.wait_ge(s["xt_lo"], QB * KT)
            for jb in range(4):
                load_vx(act, 0, jb, jb)

            def v_hi(n, jb, par, it):
                act.wait_ge(s["v"], n + 1)
                wait(act, s["o"], 4 * it - 4)
                nc.scalar.activation(V[:, par, 0, jb, :], bank[0][:], ACT.Copy).then_inc(s["v_hi"], 1)
                if not isinstance(n, int) or n + 4 < UNITS:
                    load_vx(act, it + 1, jb, n + 4)

            def qk_hi(bk, dst, pre, post, u1, hh, which):
                act.wait_ge(s[pre], u1)
                wait(act, s["s"], 4 * (u1 - 1))
                nc.scalar.activation(dst[:, 0, :], bank[bk][:], ACT.Identity, bias=bslot[:, hh, which:which + 1],
                                     scale=1.0).then_inc(s[post], 1)

            def exp_(u, qb):
                act.wait_ge(s["max"], 4 * u + (qb + 1))
                wait(act, s["t"], 4 * u)
                nc.scalar.activation(Pm[:, qb, :], bank[2 + qb % 2][:], ACT.Exp, bias=mx[:, qb:qb + 1], scale=1.0,
                                     accum_out=sm[:, qb:qb + 1]).then_inc(s["exp"], 1)

            def t_hi(u, kb):
                act.wait_ge(s["t"], 4 * u + (kb + 1))
                wait(act, s["o"], u)
                nc.scalar.activation(PT[:, 0, kb, :], bank[4 + kb % 2][:], ACT.Copy).then_inc(s["t_hi"], 1)

            def norm(u, qb):
                act.wait_ge(s["rsum"], 4 * u + (qb + 1))
                nc.scalar.activation(Pm[:, qb, :], Pm[:, qb, :], ACT.Copy, scale=ri[:, qb:qb + 1])\
                    .then_inc(s["norm_act"], 1)

            def softmax(u, others):
                exp_(u, 0)
                others()
                exp_(u, 1)
                norm(u, 0)
                exp_(u, 2)
                norm(u, 1)
                exp_(u, 3)

            for jb in range(4):
                v_hi(jb, jb, 0, 0)
            qk_hi(1, kT, "k", "k_hi", 1, 0, 1)
            qk_hi(0, qT, "q", "q_hi", 1, 0, 0)
            softmax(0, lambda: None)

            def slot(j, c):
                u = 8 * j + c
                more = not last(j, c + 1)
                if not last(j, c + 4):
                    v_hi(u + 4, c % 4, (c // 4 + 1) % 2, it_of(j, c + 4))
                t_hi(u, 0)
                t_hi(u, 1)
                if more:
                    qk_hi(1, kT, "k", "k_hi", u + 2, (c + 1) % 4, 1)
                    qk_hi(0, qT, "q", "q_hi", u + 2, (c + 1) % 4, 0)
                t_hi(u, 2)
                if more:
                    softmax(u + 1, lambda: t_hi(u, 3))
                else:
                    t_hi(u, 3)
                act.wait_ge(s["o"], u + 1)
                wait(act, s["y"], u)
                nc.scalar.activation(oT[:, 0, :], bank[1][:], ACT.Identity, bias=bslot[:, c % 4, 2:3],
                                     scale=1.0).then_inc(s["o_hi"], 1)

            slots(act, slot)

        @block.vector
        def _(dve):
            ln_steps = statistics_dve(nc, dve, m, s, None, 0)
            normalize_dve(nc, dve, m, xn, xT, s)
            dve.wait_ge(s["b_in"], 32)
            nc.vector.memset(flat, 0.0).then_inc(s["ln"], 1)
            dve.wait_ge(s["ln"], ln_steps + 1)
            for o in range(KT):
                nc.vector.tensor_scalar(yT[:, o, :], yT[:, o, :], bo[:, o:o + 1], None, ALU.add).then_inc(s["ln"], 1)
            dve.wait_ge(s["ln"], ln_steps + 1 + KT)

            def v_lo(n, jb, par):
                dve.wait_ge(s["v_hi"], n + 1)
                nc.vector.tensor_tensor(V[:, par, 1, jb, :], bank[0][:], V[:, par, 0, jb, :].bitcast(F32),
                                        ALU.subtract).then_inc(s["v_lo"], 1)

            def bias_lo(bk, dst, pre, post, u1, hh, which):
                dve.wait_ge(s[pre], u1)
                nc.vector.scalar_tensor_tensor(out=dst[:, 1, :], in0=bank[bk][:], scalar=bslot[:, hh, which:which + 1],
                                               in1=dst[:, 0, :].bitcast(F32), op0=ALU.add, op1=ALU.subtract)\
                    .then_inc(s[post], 1)

            def max_(u, qb):
                dve.wait_ge(s["s"], 4 * u + (qb + 1))
                wait(dve, s["exp"], 4 * u + qb - 3)
                nc.vector.reduce_max(mx[:, qb:qb + 1], bank[2 + qb % 2][:], AX_X, negate=True)\
                    .then_inc(s["max"], 1)

            def rsum(u, qb):
                dve.wait_ge(s["exp"], 4 * u + (qb + 1))
                wait(dve, s["norm_act"], 2 * u)
                nc.vector.reciprocal(ri[:, qb:qb + 1], sm[:, qb:qb + 1]).then_inc(s["rsum"], 1)

            def norm(u, qb):
                dve.wait_ge(s["rsum"], 4 * u + (qb + 1))
                nc.vector.tensor_scalar(Pm[:, qb, :], Pm[:, qb, :], ri[:, qb:qb + 1], None, ALU.mult)\
                    .then_inc(s["norm"], 1)

            def t_lo(u, kb):
                dve.wait_ge(s["t_hi"], 4 * u + (kb + 1))
                nc.vector.tensor_tensor(PT[:, 1, kb, :], bank[4 + kb % 2][:], PT[:, 0, kb, :].bitcast(F32),
                                        ALU.subtract).then_inc(s["t_lo"], 1)

            def y_add(it, b):
                dve.wait_ge(s["y"], 4 * it + 4)
                wait(dve, s["y_add"], it)
                for o in range(KT):
                    yo = yT[:, o, bass.ds(b * S, S)]
                    ins = nc.vector.tensor_tensor(yo, bank[6 + o][:], yo, ALU.add)
                ins.then_inc(s["y_add"], 1)

            def softmax(u, others):
                max_(u, 0)
                max_(u, 1)
                rsum(u, 0)
                others()
                max_(u, 2)
                rsum(u, 1)
                max_(u, 3)
                rsum(u, 2)
                norm(u, 2)
                rsum(u, 3)
                norm(u, 3)

            for jb in range(4):
                v_lo(jb, jb, 0)
            bias_lo(1, kT, "k_hi", "k_lo", 1, 0, 1)
            bias_lo(0, qT, "q_hi", "q_lo", 1, 0, 0)
            softmax(0, lambda: None)

            def slot(j, c):
                u = 8 * j + c
                more = not last(j, c + 1)
                if not last(j, c + 4):
                    v_lo(u + 4, c % 4, (c // 4 + 1) % 2)
                t_lo(u, 0)
                t_lo(u, 1)
                if more:
                    bias_lo(1, kT, "k_hi", "k_lo", u + 2, (c + 1) % 4, 1)
                    bias_lo(0, qT, "q_hi", "q_lo", u + 2, (c + 1) % 4, 0)
                t_lo(u, 2)
                if more:
                    softmax(u + 1, lambda: t_lo(u, 3))
                else:
                    t_lo(u, 3)
                if c % 4 == 0 and not (isinstance(j, int) and u == 0):
                    y_add(it_of(j, c - 4), batch_of(j, c - 4 + 16) if not isinstance(j, int) else (u // 4 - 1) % B)
                bias_lo(1, oT, "o_hi", "o_lo", u + 1, c % 4, 2)

            slots(dve, slot)
            y_add(UNITS // 4 - 1, B - 1)
            for i in range(NT):
                dve.wait_ge(s["fin"], i + 1)
                nc.vector.tensor_tensor(X[:, i, :], bank[i % 2][:, 0:D], X[:, i, :], ALU.add)\
                    .then_inc(s["fin_add"], 1)

        @block.tensor
        def _(pe):
            transpose_pe(nc, pe, m, xn, s)
            pe.wait_ge(s["xt_lo"], QB * KT)

            def proj(Wx, bk, hh, tok, done):
                w_ = Wx[:, hh].rearrange("p l (k n) -> p l k n", k=KT)
                product(nc, bank[bk][:], [(w_[:, 0, kt, :], w_[:, 1, kt, :], xT[:, 0, kt, bass.ds(tok, S)],
                                           xT[:, 1, kt, bass.ds(tok, S)]) for kt in range(KT)]).then_inc(s[done], 1)

            def v_block(n, jb, it):
                wait(pe, s["wprep"], (it // B) * PARTS_G + HG)
                pe.wait_ge(vx_in[jb], 16 * it + 16)
                par = (it // B) % 2
                product(nc, bank[0][:], [(vx[:, jb, 0, kt, :], vx[:, jb, 1, kt, :],
                                          *(Wv[:, bass.ds(par, 1), l, kt, :].rearrange("p a n -> p (a n)")
                                            for l in range(2))) for kt in range(KT)]).then_inc(s["v"], 1)

            def scores(u, qb):
                wait(pe, s["exp"], 4 * u + qb - 1)
                q = slice(qb * P, (qb + 1) * P)
                product(nc, bank[2 + qb % 2][:], [(qT[:, 0, q], qT[:, 1, q], kT[:, 0, :], kT[:, 1, :])])\
                    .then_inc(s["s"], 1)

            def trans(u, kb):
                wait(pe, s["t_lo"], 4 * u + kb - 1)
                for qb in range(QB):
                    ins = nc.tensor.transpose(bank[4 + kb % 2][:, qb * P:(qb + 1) * P],
                                              Pm[:, qb, kb * P:(kb + 1) * P], ident)
                ins.then_inc(s["t"], 1)

            def pv(u, kb, c):
                pe.wait_ge(s["t_lo"], 4 * u + (kb + 1))
                hh, par = c % 4, (c // 4) % 2
                vh, vl = (V[:, par, l, kb, hh * HD:(hh + 1) * HD] for l in range(2))
                ph, pl = PT[:, 0, kb, :], PT[:, 1, kb, :]
                nc.tensor.matmul(bank[1][:], vh, ph, start=(kb == 0), stop=False)
                nc.tensor.matmul(bank[1][:], vh, pl, start=False, stop=False)
                ins = nc.tensor.matmul(bank[1][:], vl, ph, start=False, stop=(kb == QB - 1))
                if kb == QB - 1:
                    ins.then_inc(s["o"], 1)

            def out_proj(u, c):
                pe.wait_ge(s["o_lo"], u + 1)
                hh = c % 4
                if hh == 0:
                    wait(pe, s["y_add"], u // 4 if isinstance(u, int) else it_now[0])
                for o in range(KT):
                    wh, wl = (Wo[:, hh, l, o * P:(o + 1) * P] for l in range(2))
                    nc.tensor.matmul(bank[6 + o][:], wh, oT[:, 0, :], start=(hh == 0), stop=False)
                    nc.tensor.matmul(bank[6 + o][:], wh, oT[:, 1, :], start=False, stop=False)
                    ins = nc.tensor.matmul(bank[6 + o][:], wl, oT[:, 0, :], start=False, stop=(hh == HG - 1))
                ins.then_inc(s["y"], 1)

            it_now = [0]
            for jb in range(4):
                wait(pe, s["v_lo"], jb)
                v_block(jb, jb, 0)
            pe.wait_ge(s["v_lo"], 4)
            pe.wait_ge(s["wprep"], HG + 3)
            proj(Wk, 1, 0, 0, "k")
            proj(Wq, 0, 0, 0, "q")
            pe.wait_ge(s["k_lo"], 1)
            pe.wait_ge(s["q_lo"], 1)
            for qb in range(QB):
                scores(0, qb)

            def slot(j, c):
                u = 8 * j + c
                more = not last(j, c + 1)
                if not last(j, c + 4):
                    pe.wait_ge(s["q_lo"], u + 1)
                    v_block(u + 4, c % 4, it_of(j, c + 4))
                pe.wait_ge(s["norm_act"], 2 * u + 2)
                pe.wait_ge(s["norm"], 2 * u + 2)
                trans(u, 0)
                trans(u, 1)
                if more:
                    hh1 = (c + 1) % 4
                    tok = batch_of(j, c + 1) * S
                    pe.wait_ge(s["wprep"], group_of(j, c + 1) * PARTS_G + (HG + 3 * hh1 + 3))
                    wait(pe, s["o_lo"], u)
                    proj(Wk, 1, hh1, tok, "k")
                    pe.wait_ge(s["v_lo"], min(u + 5, UNITS) if isinstance(u, int) else u + 5)
                    proj(Wq, 0, hh1, tok, "q")
                if not (isinstance(u, int) and u == 0):
                    it_now[0] = it_of(j, c - 1)
                    out_proj(u - 1, c - 1)
                trans(u, 2)
                if more:
                    pe.wait_ge(s["k_lo"], u + 2)
                    pe.wait_ge(s["q_lo"], u + 2)
                    scores(u + 1, 0)
                trans(u, 3)
                if more:
                    scores(u + 1, 1)
                pe.wait_ge(s["v_lo"], 4 * it_of(j, c) + 4)
                for kb in range(QB):
                    pv(u, kb, c)
                    if more and kb < 2:
                        scores(u + 1, kb + 2)

            slots(pe, slot)
            out_proj(UNITS - 1, UNITS - 1)
            pe.wait_ge(s["y_add"], UNITS // 4)
            for i in range(NT):
                wait(pe, s["fin_add"], i - 1)
                for o in range(KT):
                    ins = nc.tensor.transpose(bank[i % 2][:, o * P:(o + 1) * P], yT[:, o, i * P:(i + 1) * P], ident)
                ins.then_inc(s["fin"], 1)


def _constants(np):
    c = np.zeros((P, C_N), np.float32)
    c[:, C_ID:C_ID + P] = np.eye(P)
    c[:, C_TRI:C_TRI + P] = np.triu(np.ones((P, P)), 1)
    c[:, C_ONE:C_ONE + P] = 1.0
    c[:, C_REV:C_REV + NE] = NE - np.arange(NE)
    c[:, C_J:C_J + NE] = P * np.arange(NE)
    c[:, C_LT:C_LT + NE * NE] = np.tril(np.ones((NE, NE)), -1).reshape(-1)
    c[:, C_I:C_I + NR] = np.arange(NR)
    c[:, C_POW:C_POW + 6] = 16.0 ** np.arange(6)
    return c


def kernel(**inputs):
    import numpy as np
    import concourse.bacc as bacc
    from concourse import mybir as _mybir
    from concourse.bass_utils import run_bass_kernel_spmd

    a = {k: np.asarray(v) for k, v in inputs.items()}
    f = {k[len("L0_ffn_"):]: v for k, v in a.items() if k.startswith("L0_ffn_")}
    w = {k[len("L0_attn_"):]: v for k, v in a.items() if k.startswith("L0_attn_")}

    def rows(x):
        return x.reshape(-1, P, x.shape[-1]).transpose(1, 0, 2)

    shared = [np.concatenate([rows(f["shared_gate_w"]), rows(f["shared_up_w"])], -1).reshape(P, -1),
              rows(f["shared_down_w"]).reshape(P, -1)]
    experts = [np.concatenate([np.concatenate([rows(f["gate_w"][e]), rows(f["up_w"][e])], -1).reshape(P, -1),
                               f["down_w"][e]], -1) for e in range(NE)]

    def part(kind, h):
        cd, sc = w[f"w{kind}_codes"], w[f"w{kind}_scales"]
        if kind == "o":
            return cd[h * P:(h + 1) * P], sc[4 * h:4 * h + 4]
        return (rows(cd[:, h * HD:(h + 1) * HD]).reshape(P, -1),
                sc[:, h * HD:(h + 1) * HD].reshape(KT, 4, HD).transpose(1, 0, 2).reshape(4, -1))

    order = [("v", HG * g + i) for g in range(NG) for i in range(HG)]
    parts = []
    for g in range(NG):
        parts += [part(*o) for o in order[HG * g:HG * g + HG]]
        parts += [part(k, HG * g + i) for i in range(HG) for k in "qko"]

    arrays = {
        "x": w["x"].reshape(NTOK, D),
        "consts": _constants(np),
        "router": rows(f["router_w"].T).reshape(P, -1),
        "ffn_w": np.concatenate(shared + experts, -1),
        "codes": np.stack([p[0] for p in parts]),
        "scales": np.stack([p[1] for p in parts]),
        "attn_bias": np.concatenate([w[k].reshape(H, HD).T for k in ("bq", "bk", "bv")], -1),
        "bo": w["bo"].reshape(KT, P).T,
    }
    arrays = {k: np.ascontiguousarray(v) for k, v in arrays.items()}
    nc = bacc.Bacc("TRN2", target_bir_lowering=False, num_devices=1)
    t = {k: nc.dram_tensor(f"in_{k}", v.shape, _mybir.dt.from_np(v.dtype), kind="ExternalInput").ap()
         for k, v in arrays.items()}
    t["out"] = nc.dram_tensor("out_x", (NTOK, D), _mybir.dt.float32, kind="ExternalOutput").ap()
    build(nc, t)
    r = run_bass_kernel_spmd(nc, [{f"in_{k}": v for k, v in arrays.items()}], core_ids=[0])
    return r.results[0]["out_x"].reshape(B, S, D)
```

```python
from contextlib import ExitStack

import concourse.bass as bass
from concourse import mybir

P = 128
F32 = mybir.dt.float32
F32R = mybir.dt.float32r
BF16 = mybir.dt.bfloat16
I32 = mybir.dt.int32
ALU = mybir.AluOpType
ACT = mybir.ActivationFunctionType
AX_X = mybir.AxisListType.X

B, S, D = 4, 512, 256
NTOK = B * S
NT = NTOK // P
KT = D // P
H, HD = 16, 128
QB = S // P
NE, TOPK, FE, FS = 16, 2, 128, 256
HG = 4
NG = H // HG
UNITS = B * H
LN_EPS = 1e-5
SM_SCALE = float(HD) ** -0.5

NSLOT_TILES = (NTOK * TOPK + NE * (P - 1)) // P
NR = -(-NSLOT_TILES // 4) * 4

W_SH = KT * 2 * FS + (FS // P) * D
W_EX = KT * 2 * FE + D
W_ALL = W_SH + NE * W_EX
CHUNK = 512
NCHUNK = W_ALL // CHUNK
SH_CHUNKS = W_SH // CHUNK
FILLS = 6
FILL = NR * P // FILLS
POOL_CHUNKS = 11
FIN_BANKS = (0, 2, 3, 4, 5, 1, 6, 7)
ROW = D + 2
EARLY = 3
STEP_CHUNKS = (NCHUNK - SH_CHUNKS) // EARLY

PART = 2 * HD
PARTS_G = 4 * HG
NPARTS = NG * PARTS_G

C_ID, C_TRI, C_ONE, C_REV, C_J, C_LT, C_I = 0, 128, 256, 384, 400, 416, 672
C_POW = C_I + NR
C_N = C_POW + 8
VAR, RSTD, DELTA, HOT, TILES_KNOWN = 1, 2, 3, 4, 7


def wait(eng, sem, value):
    if isinstance(value, int) and value <= 0:
        return
    eng.wait_ge(sem, value)


class Carver:

    def __init__(self, tensor, start=0):
        self.t, self.at = tensor, start

    def cut(self, words):
        a = self.t[:, self.at:self.at + words]
        self.at += words
        return a


def build(nc, t):
    with ExitStack() as ctx:
        def sb(name, shape, dt=F32):
            return ctx.enter_context(nc.sbuf_tensor(name, shape, dt))

        m = {"ctx": ctx}
        m["X"] = sb("X", [P, NT, D])
        m["R"] = sb("R", [P, 37888], F32R)
        m["work"] = sb("work", [P, 8760])
        m["cst"] = sb("cst", [P, C_N])
        m["target"] = sb("target", [P, TOPK, NT], I32)
        m["empty"] = sb("empty", [P, ROW])
        m["tri"] = sb("tri", [P, P], BF16)
        m["one"] = sb("one", [P, P], BF16)
        m["stats"] = sb("stats", [P, NT, 6])
        m["mv"] = sb("mv", [P, NT, 2])
        m["ln"] = sb("ln", [P, 5, NT])
        m["bank"] = [ctx.enter_context(nc.psum_tensor(f"bank{i}", [P, 512], F32)) for i in range(8)]
        m["xs_dram"] = [nc.dram_tensor(f"xs_dram{f}", (NR * P, ROW), F32, kind="Internal").ap() for f in range(2)]
        m["y_dram"] = nc.dram_tensor("y_dram", (TOPK * NTOK, D), F32, kind="Internal").ap()
        ffn_phase(nc, t, m, 0)
        attention_phase(nc, t, m)
        ffn_phase(nc, t, m, 1)


def statistics_dve(nc, dve, m, s, x_ready, n):
    X, stats, mv, ln = m["X"], m["stats"], m["mv"], m["ln"]
    if x_ready != "taken":
        for i in range(NT):
            if x_ready is not None and i % QB == 0:
                dve.wait_ge(x_ready[i // QB], 16)
            nc.vector.bn_stats(stats[:, i, :], X[:, i, :]).then_inc(s["ln"], 1)
        n += NT
        dve.wait_ge(s["ln"], n)
    for i in range(NT):
        nc.vector.bn_aggr(mv[:, i, :], stats[:, i, :]).then_inc(s["ln"], 1)
    n += NT
    dve.wait_ge(s["ln"], n)
    ve, sq, r, a, b = (ln[:, i, :] for i in range(5))
    nc.vector.tensor_scalar(ve, mv[:, :, 1], LN_EPS, None, ALU.add).then_inc(s["mark"], 1)
    dve.wait_ge(s["sqrt"], 1)
    for op in (lambda: nc.vector.reciprocal(r, sq),
               lambda: nc.vector.tensor_tensor(a, ve, r, ALU.mult),
               lambda: nc.vector.tensor_tensor(b, a, r, ALU.mult),
               lambda: nc.vector.tensor_scalar(a, b, -0.5, 1.5, ALU.mult, ALU.add),
               lambda: nc.vector.tensor_tensor(b, r, a, ALU.mult)):
        op().then_inc(s["ln"], 1)
        n += 1
        dve.wait_ge(s["ln"], n)
    nc.vector.scalar_tensor_tensor(out=a, in0=mv[:, :, 0], scalar=-1.0, in1=b, op0=ALU.mult, op1=ALU.mult)\
        .then_inc(s["mark"], 1)
    return n


def normalize_dve(nc, dve, m, xn, xT, s):
    X, mv, ln = m["X"], m["mv"], m["ln"]
    for q in range(-1, QB + 1):
        if q + 1 < QB:
            for i in (4 * q + 4, 4 * q + 5):
                nc.vector.tensor_scalar(xn[:, i, :], X[:, i, :], mv[:, i, 0:1], ln[:, 4, i:i + 1],
                                        ALU.subtract, ALU.mult).then_inc(s["xn"], 1)
        if q > 0:
            for kt in range(KT):
                n = (q - 1) * KT + kt
                dve.wait_ge(s["xt_hi"], n + 1)
                part = xT[:, :, kt, (q - 1) * S:q * S]
                nc.vector.tensor_tensor(part[:, 1], m["bank"][n % 2][:], part[:, 0].bitcast(F32), ALU.subtract)\
                    .then_inc(s["xt_lo"], 1)


def normalize_act(nc, act, m, xn, xT, s, after=None, before=None):
    X, ln = m["X"], m["ln"]
    act.wait_ge(s["mark"], VAR)
    nc.scalar.activation(ln[:, 1, :], ln[:, 0, :], ACT.Sqrt).then_inc(s["sqrt"], 1)
    if before is not None:
        before()
    act.wait_ge(s["mark"], RSTD)
    for q in range(-1, QB + 1):
        if q + 1 < QB:
            for i in (4 * q + 6, 4 * q + 7):
                nc.scalar.activation(xn[:, i, :], X[:, i, :], ACT.Identity, bias=ln[:, 3, i:i + 1],
                                     scale=ln[:, 4, i:i + 1]).then_inc(s["xn_act"], 1)
        if q > 0:
            for kt in range(KT):
                n = (q - 1) * KT + kt
                act.wait_ge(s["xt"], n + 1)
                nc.scalar.activation(xT[:, 0, kt, (q - 1) * S:q * S], m["bank"][n % 2][:], ACT.Copy)\
                    .then_inc(s["xt_hi"], 1)
        if after is not None and q > 0:
            after(q)


def transpose_pe(nc, pe, m, xn, s, after=None):
    ident = m["cst"][:, C_ID:C_ID + P]
    for q in range(QB):
        pe.wait_ge(s["xn"], 2 * q + 2)
        pe.wait_ge(s["xn_act"], 2 * q + 2)
        for kt in range(KT):
            n = q * KT + kt
            wait(pe, s["xt_lo"], n - 1)
            for i in range(4):
                last = nc.tensor.transpose(m["bank"][n % 2][:, i * P:(i + 1) * P],
                                           xn[:, 4 * q + i, kt * P:(kt + 1) * P], ident)
            last.then_inc(s["xt"], 1)
        if after is not None:
            after(q)


def product(nc, out, pairs):
    n = len(pairs)
    for i, (ah, al, bh, bl) in enumerate(pairs):
        nc.tensor.matmul(out, ah, bh, start=(i == 0), stop=False)
        nc.tensor.matmul(out, ah, bl, start=False, stop=False)
        last = nc.tensor.matmul(out, al, bh, start=False, stop=(i == n - 1))
    return last


def fill_rows(eng, m, f, part, done):
    eng.dma_start(m["xs_dram"][f][bass.ds(part * FILL, FILL), :].rearrange("(n a) d -> a n d", a=P),
                  m["empty"][:].unsqueeze(1).broadcast_to([P, FILL // P, ROW])).then_inc(done, 16)


def ffn_phase(nc, t, m, f):
    X, bank, cst = m["X"], m["bank"], m["cst"]
    xs_dram, y_dram, target, empty = m["xs_dram"][f], m["y_dram"], m["target"], m["empty"]
    r = Carver(m["R"])
    W = [r.cut(W_ALL), r.cut(W_ALL)]
    xT = r.cut(2 * KT * NTOK).rearrange("p (l k n) -> p l k n", l=2, k=KT)
    small = r.at
    hT = r.cut(2 * 2 * S).rearrange("p (j l n) -> p j l n", j=2, l=2)
    r = Carver(m["R"], small)
    xsT = r.cut(2 * 2 * KT * P).rearrange("p (b l k n) -> p b l k n", b=2, l=2, k=KT)
    hrT = r.cut(2 * 2 * P).rearrange("p (b l n) -> p b l n", b=2, l=2)
    w = Carver(m["work"])
    rows = w.cut(NT * ROW).rearrange("p (t d) -> p t d", t=NT)
    xn = rows[:, :, 0:D]
    xs = rows[:, 0:8, :]
    yb = rows.rearrange("p t d -> p (t d)")[:, 0:2 * TOPK * QB * D] \
        .rearrange("p (b k t d) -> p b k (t d)", b=2, k=TOPK, t=QB)
    stage = w.cut(4 * CHUNK)
    stg = stage.rearrange("p (b n) -> p b n", b=4)
    dnb = stage[:, 0:4 * D].rearrange("p (b d) -> p b d", b=4)
    small = w.at
    sg = w.cut(2 * S).rearrange("p (j n) -> p j n", j=2)
    hf = w.cut(S)
    w = Carver(m["work"], small)
    w.cut(2 * S)
    sgr = w.cut(2 * P).rearrange("p (b n) -> p b n", b=2)
    hr = w.cut(2 * P).rearrange("p (b n) -> p b n", b=2)
    te3 = lambda a: a.rearrange("p (t e) -> p t e", t=NT)
    lgT = m["work"][0:NE, small:small + 2 * S].rearrange("e (b n) -> e b n", b=2)
    route = w.cut(4 * 256)
    L, oh1, oh2, tmp = (te3(route[:, i * 256:(i + 1) * 256]) for i in range(4))
    tec = route[0:1, 0:NR * NE].rearrange("p (i e) -> p i e", e=NE)

    with ExitStack() as ctx:
        sems = {}

        def sem(name):
            sems[name] = m["ctx"].enter_context(nc.semaphore(f"f{f}_{name}"))
            return sems[name]

        def sb(name, shape, dt=F32):
            return ctx.enter_context(nc.sbuf_tensor(f"f{f}_{name}", shape, dt))

        A = sb("A", [P, NT + 1, NE], BF16)
        rt = sb("rt", [P, 8, NT])
        pos = [sb(f"pos{k}", [P, NT], I32) for k in range(TOPK)]
        wt = [sb(f"wt{k}", [P, NT]) for k in range(TOPK)]
        rwT = sb("rwT", [P, KT, NE])
        rw = sb("rw", [P, 2, KT, NE], F32R)
        ex = sb("ex", [P, 4, NE])
        tef = sb("tef", [1, NR + 8])
        tep = sb("tep", [1, 2, NR + 4])
        pk = sb("pk", [1, 2, NR // 4 + 1])
        packed = sb("packed", [1, NR // 4 + 1], I32)
        s = sems
        x_in = [sem(f"x_in{i}") for i in range(QB)] if f == 0 else "taken"
        for name in ("cst_in", "rw_in", "zeroed", "zfill", "tri", "ln", "mark", "sqrt", "xn", "xn_act", "xt",
                     "xt_hi", "xt_lo", "rw", "lgT", "lg_sb", "logit", "rank",
                     "w_hi", "w_lo", "gu", "silu", "h", "h_hi", "h_lo", "dn", "x_add",
                     "meta", "r_xt", "r_xhi", "r_xlo", "r_gu", "r_silu", "r_h", "r_ht", "r_hhi", "r_hlo",
                     "r_dn", "r_ev0", "r_ev1", "comb"):
            if f == 0 or name not in ("cst_in", "zeroed", "zfill", "tri"):
                sem(name)
        staged = [sem(f"staged{i}") for i in range(4)]
        scat = [sem(f"scat{i}") for i in range(4)]
        ROWS_OUT = 16 * NT * TOPK // 4
        xs_in = [sem(f"xs_in{i}") for i in range(4)]
        y_in = [sem(f"y_in{i}") for i in range(2)]
        if f == 1:
            sem("out")
        block = ctx.enter_context(nc.Block())

        ident = cst[:, C_ID:C_ID + P]

        def slots(eng, slot):
            for c in range(-1, 8):
                slot(0, c)
            with eng.Fori(1, NR // 8 - 1) as j:
                for c in range(8):
                    slot(2 * j, c)
            for c in range(NR - 8, NR + 2):
                slot(0, c)

        def live(j, c):
            return not isinstance(j, int) or 0 <= 4 * j + c < NR

        def evac_dn(ns, eng, j, c):
            n = 4 * j + c
            eng.wait_ge(s["r_dn"], n + 1)
            if not (isinstance(j, int) and n < 4):
                eng.wait_ge(scat[c % 4], ROWS_OUT + 16 * (j + c // 4))
            weight = xs[:, c % 8, D + 1:D + 2]
            if ns is nc.scalar:
                ins = nc.scalar.activation(dnb[:, c % 4, :], bank[6 + c % 2][:, 0:D], ACT.Copy, scale=weight)
            else:
                ins = nc.vector.tensor_scalar(dnb[:, c % 4, :], bank[6 + c % 2][:, 0:D], weight, None, ALU.mult)
            ins.then_inc(s[f"r_ev{c % 2}"], 1)

        @block.sync
        def _(sp):
            if f == 0:
                for q in range(QB):
                    sp.dma_start(X[:, QB * q:QB * q + QB, :], t["x"][q * S:(q + 1) * S, :]
                                 .rearrange("(t p) d -> p t d", p=P)).then_inc(x_in[q], 16)
                sp.dma_start(cst[:], t["consts"]).then_inc(s["cst_in"], 16)
                sp.dma_start(target[:], t["target"].rearrange("p (k t) -> p k t", k=TOPK)).then_inc(s["cst_in"], 16)
            sp.dma_start(rwT[:], t["router"].rearrange("p (k e) -> p k e", k=KT)).then_inc(s["rw_in"], 16)

            def chunk(c, b):
                wait(sp, s["w_lo"], c - 3)
                sp.dma_start(stg[:, b, :], t["ffn_w"][:, bass.ds(c * CHUNK, CHUNK)]).then_inc(staged[b], 16)

            for c in range(4):
                chunk(c, c)
            with sp.Fori(1, NCHUNK // 4) as j:
                for b in range(4):
                    chunk(j * 4 + b, b)
            for c in range(NCHUNK // 4 * 4, NCHUNK):
                chunk(c, c % 4)

            for q in range(4):
                sp.wait_ge(scat[q], ROWS_OUT)

            def load(j, c):
                i = 4 * j + c
                if not isinstance(j, int):
                    sp.wait_ge(scat[3], ROWS_OUT)
                wait(sp, s["r_xt"], i - 3)
                if not (isinstance(j, int) and i < 8):
                    sp.wait_ge(scat[c % 4], ROWS_OUT + 16 * (j + c // 4 - 1))
                sp.dma_start(xs[:, c % 8, :], xs_dram[bass.ds(i * P, P), :]).then_inc(xs_in[c % 4], 16)

            for c in range(8):
                load(0, c)
            with sp.Fori(1, NR // 8) as j:
                for c in range(8):
                    load(2 * j, c)
            for i in range(4):
                sp.wait_ge(scat[i], ROWS_OUT + 16 * (NR // 4))
            for b in range(B):
                wait(sp, s["comb"], TOPK * (b - 1))
                for k in range(TOPK):
                    r0 = k * NTOK + b * S
                    sp.dma_start(yb[:, b % 2, k].rearrange("p (t d) -> p t d", t=QB),
                                 y_dram[r0:r0 + S, :].rearrange("(t p) d -> p t d", p=P)).then_inc(y_in[b % 2], 16)
            if f == 1:
                out_v = t["out"].rearrange("(t p) d -> p t d", p=P)
                for q in range(QB):
                    sp.wait_ge(s["comb"], TOPK * (q + 1))
                    sp.dma_start(out_v[:, 4 * q:4 * q + 4, :], X[:, 4 * q:4 * q + 4, :]).then_inc(s["out"], 16)
                sp.wait_ge(s["out"], 16 * QB)

        @block.gpsimd
        def _(pool):
            if f == 0:
                nc.gpsimd.memset(empty[:], 0.0).then_inc(s["zeroed"], 1)
                pool.wait_ge(s["zeroed"], 1)
                nc.gpsimd.memset(empty[:, D:D + 1], 1.0).then_inc(s["zeroed"], 1)
            for c in range(POOL_CHUNKS):
                pool.wait_ge(s["w_hi"], c + 1)
                cols = slice(c * CHUNK, (c + 1) * CHUNK)
                nc.gpsimd.tensor_tensor(W[1][:, cols], stg[:, c % 4, :], W[0][:, cols].bitcast(F32), ALU.subtract)\
                    .then_inc(s["w_lo"], 1)
            if f == 0:
                pool.wait_ge(s["zfill"], 16 * FILLS)
            halves = [range(0, NT // 2), range(NT // 2, NT)]

            def scatter(k, tiles, done):
                for i in tiles:
                    nc.gpsimd.indirect_dma_start(
                        out=xs_dram, out_offset=bass.IndirectOffsetOnAxis(ap=pos[k][:, i:i + 1], axis=0),
                        in_=rows[:, i, :], in_offset=None).then_inc(done, 16)

            pool.wait_ge(s["xn"], NT // 2)
            pool.wait_ge(s["xn_act"], NT // 2)
            pool.wait_ge(s["mark"], HOT + 1)
            for h in range(2):
                scatter(0, halves[h], scat[h])
            for h in range(2):
                if h == 0:
                    pool.wait_ge(s["mark"], HOT + 2)
                pool.wait_ge(scat[h], ROWS_OUT)
                tiles = slice(halves[h][0], halves[h][-1] + 1)
                nc.gpsimd.tensor_copy(rows[:, tiles, D:D + 1].bitcast(I32), target[:, 1, tiles].unsqueeze(2))\
                    .then_inc(s["meta"], 1)
                nc.gpsimd.tensor_copy(rows[:, tiles, D + 1:D + 2], wt[1][:, tiles].unsqueeze(2)).then_inc(s["meta"], 1)
                pool.wait_ge(s["meta"], 2 * h + 2)
                scatter(1, halves[h], scat[2 + h])

            last_row = pool.to_reg(TOPK * NTOK - 1)
            def results_out(j, c):
                count = 2 * j + (c // 2 + 1)
                if not isinstance(j, int):
                    count = pool.to_reg(count)
                    pool.wait_ge(s["meta"], 4)
                pool.wait_ge(s[f"r_ev{c % 2}"], count)
                nc.gpsimd.indirect_dma_start(
                    out=y_dram, out_offset=bass.IndirectOffsetOnAxis(ap=xs[:, c % 8, D:D + 1].bitcast(I32), axis=0),
                    in_=dnb[:, c % 4, :], in_offset=None, bounds_check=last_row, oob_is_err=False)\
                    .then_inc(scat[c % 4], 16)

            for c in range(8):
                results_out(0, c)
            with pool.Fori(1, NR // 8) as j:
                for c in range(8):
                    results_out(2 * j, c)

        @block.scalar
        def _(act):
            split = iter(range(NCHUNK))

            def split_hi(count):
                for _, c in zip(range(count), split):
                    act.wait_ge(staged[c % 4], 16 * (c // 4 + 1))
                    nc.scalar.activation(W[0][:, c * CHUNK:(c + 1) * CHUNK], stg[:, c % 4, :], ACT.Copy)\
                        .then_inc(s["w_hi"], 1)

            def logits_out(q):
                act.wait_ge(s["lgT"], q + 1)
                wait(act, s["logit"], q - 1)
                nc.scalar.activation(lgT[:, q % 2, :], bank[2 + 4 * (q % 2)][0:NE, :], ACT.Copy)\
                    .then_inc(s["lg_sb"], 1)

            def behind(q):
                if q <= 2:
                    split_hi(2)
                    if f == 0:
                        if q == 1:
                            act.wait_ge(s["zeroed"], 2)
                        for i in range(FILLS // 2):
                            fill_rows(act, m, 0, FILLS // 2 * (q - 1) + i, s["zfill"])
                if q >= 2:
                    logits_out(q - 2)

            def before():
                act.wait_ge(s["rw_in"], 16)
                nc.scalar.activation(rw[:, 0], rwT[:], ACT.Copy).then_inc(s["rw"], 1)
                split_hi(SH_CHUNKS)

            normalize_act(nc, act, m, xn, xT, s, behind, before)
            logits_out(QB - 1)

            act.wait_ge(s["mark"], DELTA)
            nc.scalar.activation(rt[:, 5, :], rt[:, 4, :], ACT.Exp).then_inc(s["sqrt"], 1)

            def shared(step):
                for j in range(2):
                    k = step * 2 + j
                    act.wait_ge(s["gu"], k + 1)
                    wait(act, s["h"], k - 1)
                    nc.scalar.activation(sg[:, j, :], bank[j][:], ACT.Silu).then_inc(s["silu"], 1)
                    if k == 1:
                        split_hi(3)
                    act.wait_ge(s["h"], k + 1)
                    wait(act, s["dn"], step * 4)
                    nc.scalar.activation(hT[:, j, 0, :], hf, ACT.Copy).then_inc(s["h_hi"], 1)
                    split_hi(POOL_CHUNKS - SH_CHUNKS - 4 if k == 0 else 3)

            for step in range(EARLY):
                shared(step)
            split_hi(NCHUNK)
            act.wait_ge(s["x_add"], EARLY * QB)

            def slot(j, c):
                i = 4 * j + c
                if live(j, c + 1):
                    act.wait_ge(s["r_xt"], i + 2)
                    wait(act, s["r_gu"], i)
                    nc.scalar.activation(xsT[:, (c + 1) % 2, 0].rearrange("p k n -> p (k n)"),
                                         bank[(c + 1) % 2][:, 0:D], ACT.Copy).then_inc(s["r_xhi"], 1)
                if live(j, c):
                    act.wait_ge(s["r_gu"], i + 1)
                    wait(act, s["r_h"], i - 1)
                    nc.scalar.activation(sgr[:, c % 2, :], bank[2 + c % 2][:, 0:FE], ACT.Silu)\
                        .then_inc(s["r_silu"], 1)
                if live(j, c - 1):
                    act.wait_ge(s["r_ht"], i)
                    wait(act, s["r_dn"], i - 2)
                    nc.scalar.activation(hrT[:, (c - 1) % 2, 0, :], bank[4 + (c - 1) % 2][:, 0:P], ACT.Copy)\
                        .then_inc(s["r_hhi"], 1)
                if live(j, c - 2) and c % 2 == 0:
                    evac_dn(nc.scalar, act, j, c - 2)

            slots(act, slot)
            for step in range(EARLY, QB):
                shared(step)

        @block.vector
        def _(dve):
            nc.vector.memset(A[:, 0, :], 0.0)
            nc.vector.memset(tef[:], 0.0).then_inc(s["ln"], 1)
            ln_steps = statistics_dve(nc, dve, m, s, x_in, 1)
            if f == 0:
                dve.wait_ge(s["cst_in"], 32)
                nc.vector.tensor_copy(m["tri"][:], cst[:, C_TRI:C_TRI + P])
                nc.vector.tensor_copy(m["one"][:], cst[:, C_ONE:C_ONE + P]).then_inc(s["tri"], 1)
            dve.wait_ge(s["rw"], 1)
            nc.vector.tensor_tensor(rw[:, 1], rwT[:], rw[:, 0].bitcast(F32), ALU.subtract).then_inc(s["rw"], 1)
            normalize_dve(nc, dve, m, xn, xT, s)

            split = iter(range(POOL_CHUNKS, NCHUNK))

            def split_lo(count):
                for _, c in zip(range(count), split):
                    dve.wait_ge(s["w_hi"], c + 1)
                    cols = slice(c * CHUNK, (c + 1) * CHUNK)
                    nc.vector.tensor_tensor(W[1][:, cols], stg[:, c % 4, :], W[0][:, cols].bitcast(F32),
                                            ALU.subtract).then_inc(s["w_lo"], 1)

            def shared_h(k):
                j = k % 2
                dve.wait_ge(s["silu"], k + 1)
                wait(dve, s["h_lo"], k)
                nc.vector.tensor_tensor(hf, bank[4 + j][:], sg[:, j, :], ALU.mult).then_inc(s["h"], 1)
                dve.wait_ge(s["h_hi"], k + 1)
                nc.vector.tensor_tensor(hT[:, j, 1, :], hf, hT[:, j, 0, :].bitcast(F32), ALU.subtract)\
                    .then_inc(s["h_lo"], 1)

            def shared_add(step):
                for q in range(QB):
                    dve.wait_ge(s["dn"], step * 4 + (q + 1))
                    xi = X[:, step * 4 + q, :]
                    nc.vector.scalar_tensor_tensor(out=xi, in0=bank[6 + q % 2][:, 0:D], scalar=0.5, in1=xi,
                                                   op0=ALU.mult, op1=ALU.add).then_inc(s["x_add"], 1)

            n = [ln_steps]

            def link(ins):
                ins.then_inc(s["ln"], 1)
                n[0] += 1
                dve.wait_ge(s["ln"], n[0])

            rev = cst[:, C_REV:C_REV + NE].unsqueeze(1).broadcast_to([P, NT, NE])
            m1, r1, m2, r2, dl, e2, w1 = (rt[:, i, :] for i in range(7))
            wide = lambda a: a.unsqueeze(2).broadcast_to([P, NT, NE])
            dve.wait_ge(s["logit"], QB)
            link(nc.vector.tensor_copy(L, te3(bank[3][:, 0:256])))
            link(nc.vector.reduce_max(m1, L, AX_X))
            link(nc.vector.tensor_tensor(tmp, L, wide(m1), ALU.is_equal))
            link(nc.vector.tensor_tensor(tmp, tmp, rev, ALU.mult))
            link(nc.vector.reduce_max(r1, tmp, AX_X))
            link(nc.vector.tensor_tensor(oh1, rev, wide(r1), ALU.is_equal))
            link(nc.vector.scalar_tensor_tensor(out=L, in0=oh1, scalar=-3.0e38, in1=L, op0=ALU.mult, op1=ALU.add))
            link(nc.vector.reduce_max(m2, L, AX_X))
            nc.vector.tensor_tensor(dl, m2, m1, ALU.subtract).then_inc(s["mark"], 1)
            link(nc.vector.tensor_tensor(tmp, L, wide(m2), ALU.is_equal))
            link(nc.vector.tensor_tensor(tmp, tmp, rev, ALU.mult))
            link(nc.vector.reduce_max(r2, tmp, AX_X))
            link(nc.vector.tensor_tensor(oh2, rev, wide(r2), ALU.is_equal))
            nc.vector.tensor_tensor(A[:, 1:, :], oh1, oh2, ALU.add).then_inc(s["mark"], 1)
            shared_h(0)
            dve.wait_ge(s["sqrt"], 2)
            link(nc.vector.tensor_scalar(w1, e2, 1.0, None, ALU.add))
            link(nc.vector.reciprocal(r1, w1))
            link(nc.vector.tensor_scalar(wt[0][:], r1, 0.5, None, ALU.mult))
            link(nc.vector.tensor_tensor(wt[1][:], wt[0][:], e2, ALU.mult))
            nc.vector.tensor_copy(rows[:, :, D:D + 1].bitcast(I32), target[:, 0, :].unsqueeze(2))
            link(nc.vector.tensor_copy(rows[:, :, D + 1:D + 2], wt[0][:].unsqueeze(2)))
            dve.wait_ge(s["rank"], 1)
            cnt = ex[:, 0, :]
            link(nc.vector.tensor_copy(cnt, bank[3][:, 256:256 + NE]))
            jj = cst[:, C_J:C_J + NE].unsqueeze(1).broadcast_to([P, NE, NE])
            lt = cst[:, C_LT:C_LT + NE * NE].rearrange("p (a b) -> p a b", a=NE)
            link(nc.vector.tensor_tensor(tmp, cnt.unsqueeze(2).broadcast_to([P, NE, NE]), jj, ALU.is_gt))
            link(nc.vector.reduce_sum(ex[:, 1, :], tmp, AX_X))
            link(nc.vector.tensor_tensor(tmp, ex[:, 1, :].unsqueeze(1).broadcast_to([P, NE, NE]), lt, ALU.mult))
            link(nc.vector.reduce_sum(ex[:, 2, :], tmp, AX_X))
            link(nc.vector.tensor_scalar(ex[:, 3, :], ex[:, 2, :], float(P), None, ALU.mult))
            link(nc.vector.tensor_tensor(tmp, te3(bank[3][:, 0:256]),
                                         ex[:, 3, :].unsqueeze(1).broadcast_to([P, NT, NE]), ALU.add))
            for k, oh in enumerate((oh1, oh2)):
                link(nc.vector.tensor_tensor(oh, oh, tmp, ALU.mult))
                link(nc.vector.reduce_sum(rt[:, k, :], oh, AX_X))
                nc.vector.tensor_copy(pos[k][:], rt[:, k, :]).then_inc(s["mark"], 1)
            shared_h(1)
            dve.wait_ge(s["w_lo"], POOL_CHUNKS)
            split_lo(3)
            link(nc.vector.tensor_tensor(ex[:, 0, :], ex[:, 1, :], ex[:, 2, :], ALU.add))
            link(nc.vector.tensor_tensor(tec, ex[0:1, 0, :].unsqueeze(1).broadcast_to([1, NR, NE]),
                                         cst[0:1, C_I:C_I + NR].unsqueeze(2).broadcast_to([1, NR, NE]), ALU.is_le))
            link(nc.vector.reduce_sum(tef[:, 2:2 + NR], tec, AX_X))
            link(nc.vector.tensor_scalar(tef[:, 2:2 + NR], tef[:, 2:2 + NR], float(NE - 1), None, ALU.min))
            four = lambda a: a.rearrange("p (j c) -> p j c", c=4)
            pw = cst[0:1, C_POW:C_POW + 8].unsqueeze(1).broadcast_to([1, NR // 4 + 1, 8])
            nc.vector.tensor_tensor(four(tep[:, 0, :]), four(tef[:, 2:2 + NR + 4]), pw[:, :, 0:4], ALU.mult)
            link(nc.vector.tensor_tensor(four(tep[:, 1, :]), four(tef[:, 0:NR + 4]), pw[:, :, 4:8], ALU.mult))
            link(nc.vector.reduce_sum(pk[:], tep[:].rearrange("p a (j c) -> p a j c", c=4), AX_X))
            nc.vector.tensor_tensor(packed[:], pk[:, 0, :], pk[:, 1, :], ALU.add).then_inc(s["mark"], 1)

            shared_add(0)
            split_lo(1)
            for k in range(2, 2 * EARLY):
                shared_h(k)
                split_lo(3)
                if k % 2 == 1:
                    shared_add(k // 2)
            split_lo(NCHUNK)

            def slot(j, c):
                i = 4 * j + c
                if live(j, c + 1):
                    dve.wait_ge(s["r_xhi"], i + 2)
                    nc.vector.tensor_tensor(xsT[:, (c + 1) % 2, 1].rearrange("p k n -> p (k n)"),
                                            bank[(c + 1) % 2][:, 0:D],
                                            xsT[:, (c + 1) % 2, 0].rearrange("p k n -> p (k n)").bitcast(F32),
                                            ALU.subtract).then_inc(s["r_xlo"], 1)
                if live(j, c):
                    dve.wait_ge(s["r_silu"], i + 1)
                    wait(dve, s["r_ht"], i - 1)
                    nc.vector.tensor_tensor(hr[:, c % 2, :], bank[2 + c % 2][:, FE:2 * FE], sgr[:, c % 2, :],
                                            ALU.mult).then_inc(s["r_h"], 1)
                if live(j, c - 1):
                    dve.wait_ge(s["r_hhi"], i)
                    nc.vector.tensor_tensor(hrT[:, (c - 1) % 2, 1, :], bank[4 + (c - 1) % 2][:, 0:P],
                                            hrT[:, (c - 1) % 2, 0, :].bitcast(F32), ALU.subtract)\
                        .then_inc(s["r_hlo"], 1)
                if live(j, c - 2) and c % 2 == 1:
                    evac_dn(nc.vector, dve, j, c - 2)

            slots(dve, slot)
            def combine(b):
                dve.wait_ge(y_in[b % 2], 32 * (b // 2 + 1))
                dve.wait_ge(s["x_add"], QB * (b + 1 if b >= EARLY else EARLY))
                xb = X[:, QB * b:QB * b + QB, :].rearrange("p t d -> p (t d)")
                for k in range(TOPK):
                    wait(dve, s["comb"], TOPK * b + k)
                    nc.vector.tensor_tensor(xb, yb[:, b % 2, k], xb, ALU.add).then_inc(s["comb"], 1)

            for step in range(EARLY, QB):
                shared_h(2 * step)
                shared_h(2 * step + 1)
                if step == EARLY:
                    combine(0)
                shared_add(step)
            for b in range(1, B):
                combine(b)

        @block.tensor
        def _(pe):
            if f == 0:
                pe.wait_ge(s["cst_in"], 32)

            def logits(q):
                if q == 0:
                    pe.wait_ge(s["rw"], 2)
                pe.wait_ge(s["xt_lo"], KT * q + KT)
                wait(pe, s["lg_sb"], q - 1)
                product(nc, bank[2 + 4 * (q % 2)][0:NE, :],
                        [(rw[:, 0, kt, :], rw[:, 1, kt, :], xT[:, 0, kt, q * S:(q + 1) * S],
                          xT[:, 1, kt, q * S:(q + 1) * S]) for kt in range(KT)]).then_inc(s["lgT"], 1)

            def logits_back(q):
                pe.wait_ge(s["lg_sb"], q + 1)
                for i in range(4):
                    n = 4 * q + i
                    last = nc.tensor.transpose(bank[3][:, n * NE:(n + 1) * NE], lgT[:, q % 2, i * P:(i + 1) * P],
                                               ident[0:NE, 0:NE])
                last.then_inc(s["logit"], 1)

            def behind(q):
                if q >= 1:
                    logits(q - 1)
                if q >= 3:
                    logits_back(q - 3)

            transpose_pe(nc, pe, m, xn, s, behind)
            logits(QB - 1)
            for q in range(1, QB):
                logits_back(q)

            wv = [w_[:, 0:W_SH - 2 * D].rearrange("p (k g n) -> p k g n", k=KT, g=2) for w_ in W]
            wd = [w_[:, W_SH - 2 * D:W_SH].rearrange("p (j n) -> p j n", j=2) for w_ in W]

            def gate_up(step, j):
                k = step * 2 + j
                wait(pe, s["h"], k - 1)
                for g, out in ((0, bank[j]), (1, bank[4 + j])):
                    last = product(nc, out[:], [(wv[0][:, kt, g, j * P:(j + 1) * P], wv[1][:, kt, g, j * P:(j + 1) * P],
                                                 xT[:, 0, kt, bass.ds(step * S, S)],
                                                 xT[:, 1, kt, bass.ds(step * S, S)]) for kt in range(KT)])
                last.then_inc(s["gu"], 1)

            def down(step):
                pe.wait_ge(s["h_lo"], step * 2 + 2)
                for q in range(QB):
                    wait(pe, s["x_add"], step * 4 + (q - 1))
                    product(nc, bank[6 + q % 2][:, 0:D],
                            [(hT[:, j, 0, q * P:(q + 1) * P], hT[:, j, 1, q * P:(q + 1) * P],
                              wd[0][:, j, :], wd[1][:, j, :]) for j in range(2)]).then_inc(s["dn"], 1)

            pe.wait_ge(s["w_lo"], SH_CHUNKS)
            gate_up(0, 0)
            gate_up(0, 1)
            if f == 0:
                pe.wait_ge(s["tri"], 1)
            pe.wait_ge(s["mark"], HOT)
            flatA = A[:].rearrange("p t e -> p (t e)")
            nc.tensor.matmul(bank[3][:, 0:256], m["tri"][:], flatA[:, NE:], start=True, stop=False)
            for back in range(NT - 1, 1, -1):
                nc.tensor.matmul(bank[3][:, back * NE:256], m["one"][:], flatA[:, NE:NE + 256 - back * NE],
                                 start=False, stop=False)
            nc.tensor.matmul(bank[3][:, 0:256], m["one"][:], flatA[:, 0:256], start=False, stop=True)
            for i in range(NT):
                last = nc.tensor.matmul(bank[3][:, 256:256 + NE], m["one"][:], A[:, i + 1, :],
                                        start=(i == 0), stop=(i == NT - 1))
            last.then_inc(s["rank"], 1)
            for step in range(EARLY):
                if step > 0:
                    gate_up(step, 1)
                if step + 1 < EARLY:
                    gate_up(step + 1, 0)
                down(step)

            pe.wait_ge(s["w_lo"], NCHUNK)
            pe.wait_ge(s["mark"], TILES_KNOWN)
            we = [w_[:, W_SH:W_ALL].rearrange("p (e n) -> p e n", e=NE) for w_ in W]

            words = [None]

            def slot(j, c):
                i = 4 * j + c
                if c % 8 == 0:
                    n = 2 if not isinstance(j, int) or 4 * j + c < NR else 1
                    _, words[0] = nc.values_load_multi_w_load_instructions(
                        packed[0:1, bass.ds(j + c // 4, n)], engines=[mybir.EngineType.PE],
                        min_val=0, max_val=(1 << 24) - 1)

                def expert(place):
                    return pe.snap((words[0][c % 8 // 4] >> (4 * place)) & (NE - 1), min_val=0, max_val=NE - 1)

                e_gu = expert(c % 4) if live(j, c) else None
                e_dn = expert(c % 4 + 4 if c % 4 < 2 else c % 4 - 2) if live(j, c - 2) else None
                if live(j, c):
                    pe.wait_ge(s["r_xlo"], i + 1)
                    wait(pe, s["r_h"], i - 1)
                if live(j, c + 1):
                    b = (c + 1) % 2
                    pe.wait_ge(xs_in[(c + 1) % 4], 16 * (j + (c + 1) // 4) + 16)
                    for kt in range(KT):
                        last = nc.tensor.transpose(bank[b][:, kt * P:(kt + 1) * P],
                                                   xs[:, (c + 1) % 8, kt * P:(kt + 1) * P], ident)
                    last.then_inc(s["r_xt"], 1)
                if live(j, c):
                    b = c % 2
                    gu = [[w_[:, bass.ds(e_gu, 1), kt * 2 * FE:(kt + 1) * 2 * FE].rearrange("p a n -> p (a n)")
                           for w_ in we] for kt in range(KT)]
                    product(nc, bank[2 + b][:, 0:2 * FE],
                            [(xsT[:, b, 0, kt, :], xsT[:, b, 1, kt, :], gu[kt][0], gu[kt][1])
                             for kt in range(KT)]).then_inc(s["r_gu"], 1)
                if live(j, c - 2):
                    pe.wait_ge(s["r_hlo"], i - 1)
                    wait(pe, s[f"r_ev{c % 2}"], 2 * j + (c - 2) // 2)
                if live(j, c - 1):
                    b = (c - 1) % 2
                    pe.wait_ge(s["r_h"], i)
                    nc.tensor.transpose(bank[4 + b][:, 0:P], hr[:, b, :], ident).then_inc(s["r_ht"], 1)
                if live(j, c - 2):
                    b = c % 2
                    d = [w_[:, bass.ds(e_dn, 1), KT * 2 * FE:W_EX].rearrange("p a n -> p (a n)") for w_ in we]
                    product(nc, bank[6 + b][:, 0:D], [(hrT[:, b, 0, :], hrT[:, b, 1, :], d[0], d[1])])\
                        .then_inc(s["r_dn"], 1)

            slots(pe, slot)

            for step in range(EARLY, QB):
                if step == EARLY:
                    gate_up(step, 0)
                gate_up(step, 1)
                if step + 1 < QB:
                    gate_up(step + 1, 0)
                if step == EARLY:
                    for b in range(2):
                        pe.wait_ge(s[f"r_ev{b}"], NR // 2)
                down(step)


def attention_phase(nc, t, m):
    X, bank, cst = m["X"], m["bank"], m["cst"]
    r = Carver(m["R"])
    xT = r.cut(2 * KT * NTOK).rearrange("p (l k n) -> p l k n", l=2, k=KT)
    vx = r.cut(4 * 2 * KT * P).rearrange("p (j l k n) -> p j l k n", j=4, l=2, k=KT)
    Wq, Wk, Wo = (r.cut(HG * 2 * PART).rearrange("p (h l n) -> p h l n", h=HG, l=2) for _ in range(3))
    Wv = r.cut(2 * 2 * KT * HG * HD).rearrange("p (g l k n) -> p g l k n", g=2, l=2, k=KT)
    V = r.cut(2 * 2 * QB * HG * HD).rearrange("p (i l b n) -> p i l b n", i=2, l=2, b=QB)
    qT = r.cut(2 * S).rearrange("p (l n) -> p l n", l=2)
    kT = r.cut(2 * S).rearrange("p (l n) -> p l n", l=2)
    PT = r.cut(2 * QB * S).rearrange("p (l b n) -> p l b n", l=2, b=QB)
    oT = r.cut(2 * S).rearrange("p (l n) -> p l n", l=2)
    assert r.at <= 37888
    w = Carver(m["work"])
    flat = w.cut(NT * D)
    xn = flat.rearrange("p (t d) -> p t d", t=NT)
    yT = flat.rearrange("p (o n) -> p o n", o=KT)
    Pm = w.cut(QB * S).rearrange("p (q n) -> p q n", q=QB)
    raw = w.cut(2 * 4 * PART).rearrange("p (c b n) -> p c b n", c=2, b=4)

    with ExitStack() as ctx:
        s = {}

        def sem(name):
            s[name] = m["ctx"].enter_context(nc.semaphore(f"a_{name}"))
            return s[name]

        def sb(name, shape, dt=F32):
            return ctx.enter_context(nc.sbuf_tensor(f"a_{name}", shape, dt))

        bias = sb("bias", [P, 3, H])
        bslot = sb("bslot", [P, HG, 3])
        bo = sb("bo", [P, KT])
        mx = sb("mx", [P, QB])
        sm = sb("sm", [P, QB])
        ri = sb("ri", [P, QB])
        for name in ("fill", "b_in", "ln", "mark", "sqrt", "xn", "xn_act", "xt", "xt_hi", "xt_lo", "wstep", "wprep",
                     "q", "k", "v", "s", "t", "o", "y", "q_hi", "q_lo", "k_hi", "k_lo", "v_hi", "v_lo",
                     "max", "exp", "rsum", "norm", "norm_act", "t_hi", "t_lo", "o_hi", "o_lo", "y_add", "fin", "fin_add"):
            sem(name)
        raw_in = [sem(f"raw_in{i}") for i in range(4)]
        vx_in = [sem(f"vx_in{i}") for i in range(4)]
        block = ctx.enter_context(nc.Block())
        ident = cst[:, C_ID:C_ID + P]

        LOOP0, LOOP1 = 1, UNITS // 8 - 1

        def slots(eng, slot):
            for c in range(8 * LOOP0):
                slot(0, c)
            with eng.Fori(LOOP0, LOOP1) as j:
                for c in range(8):
                    slot(j, c)
            for c in range(8 * LOOP1, UNITS):
                slot(0, c)

        def it_of(j, c):
            return 2 * j + c // 4

        def batch_of(j, c):
            return it_of(j, c) % B

        def group_of(j, c):
            return it_of(j, c) // B

        def last(j, c):
            return isinstance(j, int) and 8 * j + c >= UNITS

        def load_vx(eng, n_it, jb, n):
            wait(eng, s["v"], n - 3)
            eng.dma_start(vx[:, jb].bitcast(F32).rearrange("p l k n -> p (l k) n"),
                          xT[:, :, :, bass.ds((n_it % B) * S + jb * P, P)].bitcast(F32)
                          .rearrange("p l k n -> p (l k) n")).then_inc(vx_in[jb], 16)

        @block.sync
        def _(sp):
            sp.dma_start(bias[:], t["attn_bias"].rearrange("p (a h) -> p a h", a=3)).then_inc(s["b_in"], 16)
            sp.dma_start(bo[:], t["bo"]).then_inc(s["b_in"], 16)

            def part(j, b):
                n = 4 * j + b
                wait(sp, s["wprep"], n - 3)
                sp.dma_start(raw[:, 0, b, :], t["codes"][bass.ds(n, 1), :, :].rearrange("a p n -> (a p) n"))\
                    .then_inc(raw_in[b], 16)
                for k in range(4):
                    sp.dma_start(raw[32 * k:32 * k + 32, 1, b, :],
                                 t["scales"][bass.ds(n, 1), k, :].broadcast_to([32, PART]))\
                        .then_inc(raw_in[b], 16)

            for b in range(4):
                part(0, b)
            with sp.Fori(1, NPARTS // 4) as j:
                for b in range(4):
                    part(j, b)
            for i in range(FILLS):
                fill_rows(sp, m, 1, i, s["fill"])
            sp.wait_ge(s["fill"], 16 * FILLS)

        @block.gpsimd
        def _(pool):
            pool.wait_ge(s["b_in"], 32)
            steps = [0]

            def link(ins):
                steps[0] += 1
                ins.then_inc(s["wstep"], 1)
                pool.wait_ge(s["wstep"], steps[0])

            link(nc.gpsimd.tensor_scalar(bias[:, 0, :], bias[:, 0, :], SM_SCALE, None, ALU.mult))
            n = 0
            for g in range(NG):
                for kind, hh in [("v", i) for i in range(HG)] + [(k, i) for i in range(HG) for k in "qko"]:
                    pool.wait_ge(raw_in[n % 4], 80 * (n // 4 + 1))
                    codes, scales = raw[:, 0, n % 4, :], raw[:, 1, n % 4, :]
                    if kind == "q":
                        link(nc.gpsimd.tensor_scalar(scales, scales, SM_SCALE, None, ALU.mult))
                    link(nc.gpsimd.tensor_tensor(codes, codes, scales, ALU.mult))
                    if kind == "v":
                        wait(pool, s["v"], 16 * g - 16)
                        hi, lo = (Wv[:, g % 2, l, :, hh * HD:(hh + 1) * HD] for l in range(2))
                        src = codes.rearrange("p (k n) -> p k n", k=KT)
                    else:
                        slot = {"q": Wq, "k": Wk, "o": Wo}[kind]
                        hi, lo = slot[:, hh, 0, :], slot[:, hh, 1, :]
                        src = codes
                        if kind in "qk":
                            wait(pool, s["k_lo"], 16 * g - 3 + hh)
                            if kind == "q" and g > 0:
                                pool.wait_ge(s["y"], 16 * g - 3 + hh)
                        else:
                            wait(pool, s["y"], 16 * g - 3 + hh)
                    if kind == "q":
                        link(nc.gpsimd.tensor_copy(bslot[:, hh, :], bias[:, :, 4 * g + hh]))
                    link(nc.gpsimd.tensor_copy(hi, src))
                    nc.gpsimd.tensor_tensor(lo, src, hi.bitcast(F32), ALU.subtract).then_inc(s["wprep"], 1)
                    n += 1

        @block.scalar
        def _(act):
            normalize_act(nc, act, m, xn, xT, s)
            act.wait_ge(s["xt_lo"], QB * KT)

            def v_hi(n, jb, par, it, bk=0):
                act.wait_ge(s["v"], n + 1)
                wait(act, s["o"], 4 * it - 4)
                nc.scalar.activation(V[:, par, 0, jb, :], bank[bk][:], ACT.Copy).then_inc(s["v_hi"], 1)
                if not isinstance(n, int) or n + 4 < UNITS:
                    load_vx(act, it + 1, jb, n + 4)

            def qk_hi(bk, dst, pre, post, u1, hh, which):
                act.wait_ge(s[pre], u1)
                wait(act, s["s"], 4 * (u1 - 1))
                nc.scalar.activation(dst[:, 0, :], bank[bk][:], ACT.Identity, bias=bslot[:, hh, which:which + 1],
                                     scale=1.0).then_inc(s[post], 1)

            def exp_(u, qb):
                act.wait_ge(s["max"], 4 * u + (qb + 1))
                wait(act, s["t"], 4 * u)
                nc.scalar.activation(Pm[:, qb, :], bank[2 + qb % 2][:], ACT.Exp, bias=mx[:, qb:qb + 1], scale=1.0,
                                     accum_out=sm[:, qb:qb + 1]).then_inc(s["exp"], 1)

            def t_hi(u, kb):
                act.wait_ge(s["t"], 4 * u + (kb + 1))
                wait(act, s["o"], u)
                nc.scalar.activation(PT[:, 0, kb, :], bank[4 + kb % 2][:], ACT.Copy).then_inc(s["t_hi"], 1)

            def norm(u, qb):
                act.wait_ge(s["rsum"], 4 * u + (qb + 1))
                nc.scalar.activation(Pm[:, qb, :], Pm[:, qb, :], ACT.Copy, scale=ri[:, qb:qb + 1])\
                    .then_inc(s["norm_act"], 1)

            def softmax(u):
                exp_(u, 0)
                exp_(u, 1)
                norm(u, 0)
                norm(u, 1)
                exp_(u, 2)
                exp_(u, 3)

            for jb in range(4):
                v_hi(jb, jb, 0, 0, 4 + jb)
            qk_hi(1, kT, "k", "k_hi", 1, 0, 1)
            qk_hi(0, qT, "q", "q_hi", 1, 0, 0)
            softmax(0)

            def slot(j, c):
                u = 8 * j + c
                more = not last(j, c + 1)
                if not last(j, c + 4):
                    v_hi(u + 4, c % 4, (c // 4 + 1) % 2, it_of(j, c + 4))
                t_hi(u, 0)
                t_hi(u, 1)
                if more:
                    qk_hi(1, kT, "k", "k_hi", u + 2, (c + 1) % 4, 1)
                    qk_hi(0, qT, "q", "q_hi", u + 2, (c + 1) % 4, 0)
                t_hi(u, 2)
                t_hi(u, 3)
                if more:
                    softmax(u + 1)
                act.wait_ge(s["o"], u + 1)
                wait(act, s["y"], u)
                nc.scalar.activation(oT[:, 0, :], bank[1][:], ACT.Identity, bias=bslot[:, c % 4, 2:3],
                                     scale=1.0).then_inc(s["o_hi"], 1)

            slots(act, slot)

        @block.vector
        def _(dve):
            ln_steps = statistics_dve(nc, dve, m, s, None, 0)
            normalize_dve(nc, dve, m, xn, xT, s)
            def y_start(b):
                if b == 0:
                    dve.wait_ge(s["b_in"], 32)
                for o in range(KT):
                    nc.vector.tensor_copy(yT[:, o, b * S:(b + 1) * S], bo[:, o:o + 1].broadcast_to([P, S]))\
                        .then_inc(s["ln"], 1)

            def v_lo(n, jb, par, bk=0):
                dve.wait_ge(s["v_hi"], n + 1)
                nc.vector.tensor_tensor(V[:, par, 1, jb, :], bank[bk][:], V[:, par, 0, jb, :].bitcast(F32),
                                        ALU.subtract).then_inc(s["v_lo"], 1)

            def bias_lo(bk, dst, pre, post, u1, hh, which):
                dve.wait_ge(s[pre], u1)
                nc.vector.scalar_tensor_tensor(out=dst[:, 1, :], in0=bank[bk][:], scalar=bslot[:, hh, which:which + 1],
                                               in1=dst[:, 0, :].bitcast(F32), op0=ALU.add, op1=ALU.subtract)\
                    .then_inc(s[post], 1)

            def max_(u, qb):
                dve.wait_ge(s["s"], 4 * u + (qb + 1))
                wait(dve, s["exp"], 4 * u + qb - 3)
                nc.vector.reduce_max(mx[:, qb:qb + 1], bank[2 + qb % 2][:], AX_X, negate=True)\
                    .then_inc(s["max"], 1)

            def rsum(u, qb):
                dve.wait_ge(s["exp"], 4 * u + (qb + 1))
                wait(dve, s["norm_act"], 2 * u)
                nc.vector.reciprocal(ri[:, qb:qb + 1], sm[:, qb:qb + 1]).then_inc(s["rsum"], 1)

            def norm(u, qb):
                dve.wait_ge(s["rsum"], 4 * u + (qb + 1))
                nc.vector.tensor_scalar(Pm[:, qb, :], Pm[:, qb, :], ri[:, qb:qb + 1], None, ALU.mult)\
                    .then_inc(s["norm"], 1)

            def t_lo(u, kb):
                dve.wait_ge(s["t_hi"], 4 * u + (kb + 1))
                nc.vector.tensor_tensor(PT[:, 1, kb, :], bank[4 + kb % 2][:], PT[:, 0, kb, :].bitcast(F32),
                                        ALU.subtract).then_inc(s["t_lo"], 1)

            def y_add(it, b):
                dve.wait_ge(s["y"], 4 * it + 4)
                wait(dve, s["y_add"], it)
                for o in range(KT):
                    yo = yT[:, o, bass.ds(b * S, S)]
                    ins = nc.vector.tensor_tensor(yo, bank[6 + o][:], yo, ALU.add)
                ins.then_inc(s["y_add"], 1)

            def softmax(u, behind):
                max_(u, 0)
                max_(u, 1)
                behind(2)
                rsum(u, 0)
                behind(3)
                rsum(u, 1)
                max_(u, 2)
                max_(u, 3)
                for qb in range(2, QB):
                    rsum(u, qb)
                    norm(u, qb)

            for jb in range(4):
                v_lo(jb, jb, 0, 4 + jb)
            bias_lo(1, kT, "k_hi", "k_lo", 1, 0, 1)
            bias_lo(0, qT, "q_hi", "q_lo", 1, 0, 0)
            softmax(0, lambda kb: None)

            def slot(j, c):
                u = 8 * j + c
                more = not last(j, c + 1)
                if not last(j, c + 4):
                    v_lo(u + 4, c % 4, (c // 4 + 1) % 2)
                t_lo(u, 0)
                t_lo(u, 1)
                if more:
                    bias_lo(1, kT, "k_hi", "k_lo", u + 2, (c + 1) % 4, 1)
                    bias_lo(0, qT, "q_hi", "q_lo", u + 2, (c + 1) % 4, 0)
                if more:
                    softmax(u + 1, lambda kb: t_lo(u, kb))
                else:
                    t_lo(u, 2)
                    t_lo(u, 3)
                if isinstance(u, int) and u < B:
                    y_start(u)
                if isinstance(u, int) and u == B:
                    dve.wait_ge(s["ln"], ln_steps + B * KT)
                if c % 4 == 0 and not (isinstance(j, int) and u == 0):
                    y_add(it_of(j, c - 4), batch_of(j, c - 4 + 16) if not isinstance(j, int) else (u // 4 - 1) % B)
                bias_lo(1, oT, "o_hi", "o_lo", u + 1, c % 4, 2)

            slots(dve, slot)
            def fin_add(pair):
                dve.wait_ge(s["fin"], pair + 1)
                xp = X[:, 2 * pair:2 * pair + 2, :].rearrange("p t d -> p (t d)")
                nc.vector.tensor_tensor(xp, bank[FIN_BANKS[pair]][:], xp, ALU.add).then_inc(s["fin_add"], 1)

            def statistics(pair):
                dve.wait_ge(s["fin_add"], pair + 1)
                for i in (2 * pair, 2 * pair + 1):
                    nc.vector.bn_stats(m["stats"][:, i, :], X[:, i, :])

            for pair in range(5):
                fin_add(pair)
            y_add(UNITS // 4 - 1, B - 1)
            fin_add(5)
            statistics(0)
            fin_add(6)
            fin_add(7)
            for pair in range(1, NT // 2):
                statistics(pair)

        @block.tensor
        def _(pe):
            transpose_pe(nc, pe, m, xn, s)
            pe.wait_ge(s["xt_lo"], QB * KT)

            def proj(Wx, bk, hh, tok, done):
                w_ = Wx[:, hh].rearrange("p l (k n) -> p l k n", k=KT)
                product(nc, bank[bk][:], [(w_[:, 0, kt, :], w_[:, 1, kt, :], xT[:, 0, kt, bass.ds(tok, S)],
                                           xT[:, 1, kt, bass.ds(tok, S)]) for kt in range(KT)]).then_inc(s[done], 1)

            def v_block(n, jb, it):
                wait(pe, s["wprep"], (it // B) * PARTS_G + HG)
                if isinstance(it, int) and it == 0:
                    x_, out = xT[:, :, :, jb * P:(jb + 1) * P], bank[4 + jb]
                else:
                    pe.wait_ge(vx_in[jb], 16 * it)
                    x_, out = vx[:, jb], bank[0]
                par = (it // B) % 2
                product(nc, out[:], [(x_[:, 0, kt, :], x_[:, 1, kt, :],
                                          *(Wv[:, bass.ds(par, 1), l, kt, :].rearrange("p a n -> p (a n)")
                                            for l in range(2))) for kt in range(KT)]).then_inc(s["v"], 1)

            def scores(u, qb):
                wait(pe, s["exp"], 4 * u + qb - 1)
                q = slice(qb * P, (qb + 1) * P)
                product(nc, bank[2 + qb % 2][:], [(qT[:, 0, q], qT[:, 1, q], kT[:, 0, :], kT[:, 1, :])])\
                    .then_inc(s["s"], 1)

            def trans(u, kb):
                wait(pe, s["t_lo"], 4 * u + kb - 1)
                for qb in range(QB):
                    ins = nc.tensor.transpose(bank[4 + kb % 2][:, qb * P:(qb + 1) * P],
                                              Pm[:, qb, kb * P:(kb + 1) * P], ident)
                ins.then_inc(s["t"], 1)

            def pv(u, kb, c):
                pe.wait_ge(s["t_lo"], 4 * u + (kb + 1))
                hh, par = c % 4, (c // 4) % 2
                vh, vl = (V[:, par, l, kb, hh * HD:(hh + 1) * HD] for l in range(2))
                ph, pl = PT[:, 0, kb, :], PT[:, 1, kb, :]
                nc.tensor.matmul(bank[1][:], vh, ph, start=(kb == 0), stop=False)
                nc.tensor.matmul(bank[1][:], vh, pl, start=False, stop=False)
                ins = nc.tensor.matmul(bank[1][:], vl, ph, start=False, stop=(kb == QB - 1))
                if kb == QB - 1:
                    ins.then_inc(s["o"], 1)

            def out_proj(u, c):
                pe.wait_ge(s["o_lo"], u + 1)
                hh = c % 4
                if hh == 0:
                    wait(pe, s["y_add"], u // 4 if isinstance(u, int) else it_now[0])
                for o in range(KT):
                    wh, wl = (Wo[:, hh, l, o * P:(o + 1) * P] for l in range(2))
                    nc.tensor.matmul(bank[6 + o][:], wh, oT[:, 0, :], start=(hh == 0), stop=False)
                    nc.tensor.matmul(bank[6 + o][:], wh, oT[:, 1, :], start=False, stop=False)
                    ins = nc.tensor.matmul(bank[6 + o][:], wl, oT[:, 0, :], start=False, stop=(hh == HG - 1))
                ins.then_inc(s["y"], 1)

            it_now = [0]
            for jb in range(4):
                v_block(jb, jb, 0)
            pe.wait_ge(s["wprep"], HG + 3)
            proj(Wk, 1, 0, 0, "k")
            proj(Wq, 0, 0, 0, "q")
            pe.wait_ge(s["k_lo"], 1)
            pe.wait_ge(s["q_lo"], 1)
            for qb in range(QB):
                scores(0, qb)

            def slot(j, c):
                u = 8 * j + c
                more = not last(j, c + 1)
                if not last(j, c + 4):
                    pe.wait_ge(s["q_lo"], u + 1)
                    v_block(u + 4, c % 4, it_of(j, c + 4))
                pe.wait_ge(s["norm_act"], 2 * u + 2)
                pe.wait_ge(s["norm"], 2 * u + 2)
                trans(u, 0)
                trans(u, 1)
                if more:
                    hh1 = (c + 1) % 4
                    tok = batch_of(j, c + 1) * S
                    pe.wait_ge(s["wprep"], group_of(j, c + 1) * PARTS_G + (HG + 3 * hh1 + 3))
                    wait(pe, s["o_lo"], u)
                    proj(Wk, 1, hh1, tok, "k")
                    pe.wait_ge(s["v_lo"], min(u + 5, UNITS) if isinstance(u, int) else u + 5)
                    proj(Wq, 0, hh1, tok, "q")
                if not (isinstance(u, int) and u == 0):
                    it_now[0] = it_of(j, c - 1)
                    out_proj(u - 1, c - 1)
                trans(u, 2)
                trans(u, 3)
                if more:
                    pe.wait_ge(s["k_lo"], u + 2)
                    pe.wait_ge(s["q_lo"], u + 2)
                    scores(u + 1, 0)
                    scores(u + 1, 1)
                pe.wait_ge(s["v_lo"], 4 * it_of(j, c) + 4)
                for kb in range(QB):
                    pv(u, kb, c)
                    if more and kb == 1:
                        scores(u + 1, 2)
                        scores(u + 1, 3)

            slots(pe, slot)
            def back(pair):
                for i in (2 * pair, 2 * pair + 1):
                    for o in range(KT):
                        at = (i % 2 * KT + o) * P
                        ins = nc.tensor.transpose(bank[FIN_BANKS[pair]][:, at:at + P], yT[:, o, i * P:(i + 1) * P],
                                                  ident)
                ins.then_inc(s["fin"], 1)

            pe.wait_ge(s["y_add"], UNITS // 4 - 1)
            pe.wait_ge(s["exp"], 4 * UNITS)
            for pair in range(5):
                back(pair)
            out_proj(UNITS - 1, UNITS - 1)
            back(5)
            pe.wait_ge(s["y_add"], UNITS // 4)
            back(6)
            back(7)


def _constants(np):
    c = np.zeros((P, C_N), np.float32)
    c[:, C_ID:C_ID + P] = np.eye(P)
    c[:, C_TRI:C_TRI + P] = np.triu(np.ones((P, P)), 1)
    c[:, C_ONE:C_ONE + P] = 1.0
    c[:, C_REV:C_REV + NE] = NE - np.arange(NE)
    c[:, C_J:C_J + NE] = P * np.arange(NE)
    c[:, C_LT:C_LT + NE * NE] = np.tril(np.ones((NE, NE)), -1).reshape(-1)
    c[:, C_I:C_I + NR] = np.arange(NR)
    c[:, C_POW:C_POW + 6] = 16.0 ** np.arange(6)
    return c


def kernel(**inputs):
    import numpy as np
    import concourse.bacc as bacc
    from concourse import mybir as _mybir
    from concourse.bass_utils import run_bass_kernel_spmd

    a = {k: np.asarray(v) for k, v in inputs.items()}
    f = {k[len("L0_ffn_"):]: v for k, v in a.items() if k.startswith("L0_ffn_")}
    w = {k[len("L0_attn_"):]: v for k, v in a.items() if k.startswith("L0_attn_")}

    def rows(x):
        return x.reshape(-1, P, x.shape[-1]).transpose(1, 0, 2)

    shared = [np.concatenate([rows(f["shared_gate_w"]), rows(f["shared_up_w"])], -1).reshape(P, -1),
              rows(f["shared_down_w"]).reshape(P, -1)]
    experts = [np.concatenate([np.concatenate([rows(f["gate_w"][e]), rows(f["up_w"][e])], -1).reshape(P, -1),
                               f["down_w"][e]], -1) for e in range(NE)]

    def part(kind, h):
        cd, sc = w[f"w{kind}_codes"], w[f"w{kind}_scales"]
        if kind == "o":
            return cd[h * P:(h + 1) * P], sc[4 * h:4 * h + 4]
        return (rows(cd[:, h * HD:(h + 1) * HD]).reshape(P, -1),
                sc[:, h * HD:(h + 1) * HD].reshape(KT, 4, HD).transpose(1, 0, 2).reshape(4, -1))

    order = [("v", HG * g + i) for g in range(NG) for i in range(HG)]
    parts = []
    for g in range(NG):
        parts += [part(*o) for o in order[HG * g:HG * g + HG]]
        parts += [part(k, HG * g + i) for i in range(HG) for k in "qko"]

    arrays = {
        "x": w["x"].reshape(NTOK, D),
        "consts": _constants(np),
        "target": (np.arange(TOPK)[None, :, None] * NTOK + np.arange(NT)[None, None, :] * P
                   + np.arange(P)[:, None, None]).astype(np.int32).reshape(P, -1),
        "router": rows(f["router_w"].T).reshape(P, -1),
        "ffn_w": np.concatenate(shared + experts, -1),
        "codes": np.stack([p[0] for p in parts]),
        "scales": np.stack([p[1] for p in parts]),
        "attn_bias": np.concatenate([w[k].reshape(H, HD).T for k in ("bq", "bk", "bv")], -1),
        "bo": w["bo"].reshape(KT, P).T,
    }
    arrays = {k: np.ascontiguousarray(v) for k, v in arrays.items()}
    nc = bacc.Bacc("TRN2", target_bir_lowering=False, num_devices=1)
    t = {k: nc.dram_tensor(f"in_{k}", v.shape, _mybir.dt.from_np(v.dtype), kind="ExternalInput").ap()
         for k, v in arrays.items()}
    t["out"] = nc.dram_tensor("out_x", (NTOK, D), _mybir.dt.float32, kind="ExternalOutput").ap()
    build(nc, t)
    r = run_bass_kernel_spmd(nc, [{f"in_{k}": v for k, v in arrays.items()}], core_ids=[0])
    return r.results[0]["out_x"].reshape(B, S, D)
```
